# Optimizing a Trainium2 kernel written in Bass

```python
import numpy as np
import jax
import jax.numpy as jnp

def _softmax(x, axis=-1):
    return jax.nn.softmax(x, axis=axis)

def _gelu(x):
    return jax.nn.gelu(x, approximate=True)

def _silu(x):
    return jax.nn.silu(x)

def _sigmoid(x):
    return jax.nn.sigmoid(x)

def _layernorm(x, axis=-1, eps=1e-05):
    m = jnp.mean(x, axis=axis, keepdims=True)
    v = jnp.var(x, axis=axis, keepdims=True)
    return (x - m) / jnp.sqrt(v + eps)

def _scatter_add(tgt, idx, src, axis=0):
    return tgt.at[idx].add(src)

def _segment_sum(src, seg, n):
    return jax.ops.segment_sum(src, seg, n)
kernel_name = 'mk_seq_postln_d1_jaxref_r8_1ad984'

def setup_inputs(seed: int=0):
    np.random.seed(seed)
    _w = jnp.asarray

    def _L0_attn_setup():
        import jax, jax.numpy as jnp
        import numpy as np
        D_MODEL = 256
        N_HEADS = 32
        N_KV_HEADS = 8
        HEAD_DIM = D_MODEL // N_HEADS
        ROPE_BASE = 10000.0

        def _rope_cos_sin(seq_len, dtype):
            inv_freq = 1.0 / ROPE_BASE ** (jnp.arange(0, HEAD_DIM, 2, dtype=jnp.float32) / HEAD_DIM)
            t = jnp.arange(seq_len, dtype=jnp.float32)
            freqs = jnp.einsum('i,j->ij', t, inv_freq)
            emb = jnp.concatenate([freqs, freqs], axis=-1)
            return (jnp.cos(emb).astype(dtype), jnp.sin(emb).astype(dtype))

        def _rotate_half(x):
            x1, x2 = (x[..., :HEAD_DIM // 2], x[..., HEAD_DIM // 2:])
            return jnp.concatenate([-x2, x1], axis=-1)
        key = jax.random.key(seed)
        ks = jax.random.split(key, 5)
        B, S = (1, 256)
        x = jax.random.normal(ks[0], (B, S, D_MODEL), dtype=jnp.float32)
        sc = 1.0 / np.sqrt(D_MODEL)
        Wq = jax.random.normal(ks[1], (D_MODEL, D_MODEL), dtype=jnp.float32) * sc
        Wk = jax.random.normal(ks[2], (N_KV_HEADS * HEAD_DIM, D_MODEL), dtype=jnp.float32) * sc
        Wv = jax.random.normal(ks[3], (N_KV_HEADS * HEAD_DIM, D_MODEL), dtype=jnp.float32) * sc
        Wo = jax.random.normal(ks[4], (D_MODEL, D_MODEL), dtype=jnp.float32) * sc
        return {'x': x, 'Wq': Wq, 'Wk': Wk, 'Wv': Wv, 'Wo': Wo}
    _L0_attn_in = _L0_attn_setup()

    def _L0_ffn_setup():
        import jax, jax.numpy as jnp
        import numpy as np

        def _sparsify_2to4(h):
            B, S, I = h.shape
            g = h.reshape(B, S, I // 4, 4)
            a = jnp.abs(g)
            _, idx = jax.lax.top_k(a, 2)
            pos = jnp.arange(4)
            mask = (pos == idx[..., 0:1]) | (pos == idx[..., 1:2])
            return (g * mask.astype(g.dtype)).reshape(B, S, I)
        key = jax.random.key(seed)
        k1, k2, k3, k4 = jax.random.split(key, 4)
        B, S, H, I = (4, 256, 256, 1024)
        x = jax.random.normal(k1, (B, S, H), dtype=jnp.float32)
        w_gate = jax.random.normal(k2, (H, I), dtype=jnp.float32) / np.sqrt(H)
        w_up = jax.random.normal(k3, (H, I), dtype=jnp.float32) / np.sqrt(H)
        w_down = jax.random.normal(k4, (I, H), dtype=jnp.float32) / np.sqrt(I)
        return {'x': x, 'w_gate': w_gate, 'w_up': w_up, 'w_down': w_down}
    _L0_ffn_in = _L0_ffn_setup()
    _d = {'L0_attn_x': _L0_attn_in['x'], 'L0_attn_Wq': _L0_attn_in['Wq'], 'L0_attn_Wk': _L0_attn_in['Wk'], 'L0_attn_Wv': _L0_attn_in['Wv'], 'L0_attn_Wo': _L0_attn_in['Wo'], 'L0_ffn_w_gate': _L0_ffn_in['w_gate'], 'L0_ffn_w_up': _L0_ffn_in['w_up'], 'L0_ffn_w_down': _L0_ffn_in['w_down']}
    _x0 = _d['L0_attn_x']
    _d['L0_attn_x'] = jax.random.normal(jax.random.fold_in(jax.random.key(seed), 1), (8, 512, 256), dtype=_x0.dtype)
    del _x0
    return _d

def reference(L0_attn_x, L0_attn_Wq, L0_attn_Wk, L0_attn_Wv, L0_attn_Wo, L0_ffn_w_gate, L0_ffn_w_up, L0_ffn_w_down):

    def _L0_attn_ref(x, Wq, Wk, Wv, Wo):
        import jax, jax.numpy as jnp
        import numpy as np
        D_MODEL = 256
        N_HEADS = 32
        N_KV_HEADS = 8
        HEAD_DIM = D_MODEL // N_HEADS
        ROPE_BASE = 10000.0

        def _rope_cos_sin(seq_len, dtype):
            inv_freq = 1.0 / ROPE_BASE ** (jnp.arange(0, HEAD_DIM, 2, dtype=jnp.float32) / HEAD_DIM)
            t = jnp.arange(seq_len, dtype=jnp.float32)
            freqs = jnp.einsum('i,j->ij', t, inv_freq)
            emb = jnp.concatenate([freqs, freqs], axis=-1)
            return (jnp.cos(emb).astype(dtype), jnp.sin(emb).astype(dtype))

        def _rotate_half(x):
            x1, x2 = (x[..., :HEAD_DIM // 2], x[..., HEAD_DIM // 2:])
            return jnp.concatenate([-x2, x1], axis=-1)
        B, S, _ = x.shape
        scale = HEAD_DIM ** (-0.5)
        q = (x @ Wq.T).reshape(B, S, N_HEADS, HEAD_DIM).transpose(0, 2, 1, 3)
        k = (x @ Wk.T).reshape(B, S, N_KV_HEADS, HEAD_DIM).transpose(0, 2, 1, 3)
        v = (x @ Wv.T).reshape(B, S, N_KV_HEADS, HEAD_DIM).transpose(0, 2, 1, 3)
        cos, sin = _rope_cos_sin(S, x.dtype)
        q = q * cos + _rotate_half(q) * sin
        k = k * cos + _rotate_half(k) * sin
        rep = N_HEADS // N_KV_HEADS
        k = jnp.repeat(k, rep, axis=1)
        v = jnp.repeat(v, rep, axis=1)
        scores = jnp.einsum('bhqd,bhkd->bhqk', q, k) * scale
        attn = jax.nn.softmax(scores, axis=-1)
        out = jnp.einsum('bhqk,bhkd->bhqd', attn, v)
        out = out.transpose(0, 2, 1, 3).reshape(B, S, D_MODEL)
        return out @ Wo.T

    def _L0_ffn_ref(x, w_gate, w_up, w_down):
        import jax, jax.numpy as jnp
        import numpy as np

        def _sparsify_2to4(h):
            B, S, I = h.shape
            g = h.reshape(B, S, I // 4, 4)
            a = jnp.abs(g)
            _, idx = jax.lax.top_k(a, 2)
            pos = jnp.arange(4)
            mask = (pos == idx[..., 0:1]) | (pos == idx[..., 1:2])
            return (g * mask.astype(g.dtype)).reshape(B, S, I)
        h = jax.nn.silu(jnp.einsum('bsh,hi->bsi', x, w_gate)) * jnp.einsum('bsh,hi->bsi', x, w_up)
        h_sparse = _sparsify_2to4(h)
        return jnp.einsum('bsi,ih->bsh', h_sparse, w_down)
    x = L0_attn_x
    x = _layernorm(x + _L0_attn_ref(x, L0_attn_Wq, L0_attn_Wk, L0_attn_Wv, L0_attn_Wo), axis=-1)
    x = _layernorm(x + _L0_ffn_ref(x, L0_ffn_w_gate, L0_ffn_w_up, L0_ffn_w_down), axis=-1)
    return x

_drawn_inputs = setup_inputs


def setup_inputs(seed=0):
    import zlib

    import numpy as np

    out = dict(_drawn_inputs(seed))
    spreads = {}
    factors = {}
    for name, (base, spread) in spreads.items():
        noise = np.random.default_rng([zlib.crc32(name.encode()), seed]).standard_normal(out[name].shape)
        drawn = base * np.exp(spread * noise) if base else spread * noise
        out[name] = jnp.asarray(drawn.astype(out[name].dtype))
    for name, factor in factors.items():
        out[name] = (out[name] * factor).astype(out[name].dtype)
    return out
```

```python
from contextlib import ExitStack

import numpy as np

import concourse.bass as bass
from concourse import mybir

F32 = mybir.dt.float32
BF16 = mybir.dt.bfloat16
ALU = mybir.AluOpType
ACT = mybir.ActivationFunctionType
AX = mybir.AxisListType

P = 128
B, S, D = 8, 512, 256
H, KV, HD = 32, 8, 8
I = 1024
TT = S // P
KC = D // P
QK = (H + KV) * HD
QKV = QK + KV * HD
GROUPS = H // 4
SLOTS = H
PARTS = 3
AUG = 96
SCALE = HD ** -0.5
EPS = 1e-5
SB = 3

MB_USES = [
    ((2, 0), "ott7", "F"), ((3, 1), "qkv0", "A"), ((4, 0), "oT0", "F"), ((4, 1), "qkv1", "A"),
    ((5, 0), "oT1", "F"), ((5, 1), "mt1", "B"), ((6, 0), "ott0", "B"), ((6, 1), "qkv2", "A"),
    ((8, 1), "qkv3", "A"), ((10, 0), "ott1", "B"), ((11, 0), "xT0", "F"), ((12, 0), "xT1", "F"),
    ((14, 0), "ott2", "B"), ((18, 0), "ott3", "B"), ((19, 0), "pT0", "A"), ((21, 0), "pT1", "A"),
    ((21, 1), "mt0", "M"), ((22, 0), "ott4", "B"), ((23, 1), "pT2", "A"), ((25, 0), "pT3", "A"),
    ((25, 1), "pT4", "A"), ((26, 0), "ott5", "B"), ((30, 0), "ott6", "B"),
]
MA_USES = ([((7, 0), "wo0"), ((8, 0), "wo1")] + [((13 + f // 2, f % 2), f"gu{f}") for f in range(16)]
           + [((23, 0), "dn0"), ((24, 0), "dn1"), ((27, 0), "dn2"), ((28, 0), "dn3")])
MA_FILLS = [n for _, n in MA_USES if n not in ("dn0", "dn2")]
PT_ORDER = [(0, 0), (1, 0), (2, 0), (0, 2), (1, 2), (2, 2), (0, 1), (1, 1), (2, 1)]
LAG = {"A": 2, "M": 1, "B": 0, "F": -1}


class Batch:

    def __init__(self, first, r=None, stride=2):
        self.first, self.r, self.stride = first, r, stride

    def plus(self, n):
        return Batch(self.first + n, self.r, self.stride)

    @property
    def real(self):
        return self.r is not None or 0 <= self.first < B

    @property
    def parity(self):
        return self.first % 2

    def count(self, per, more):
        v = self.first * per + more
        return max(v, 0) if self.r is None else v + self.r * (self.stride * per)

    @property
    def index(self):
        return self.count(1, 0)


def mb_count(step, name):
    n = 0
    for stage in "AMBF":
        per = sum(1 for _, _, s in MB_USES if s == stage)
        b = step.plus(LAG[stage])
        n = n + (b.count(per, 0) if step.r is not None else per * min(max(b.first, 0), B))
    here = 0
    for _, use, stage in MB_USES:
        if step.plus(LAG[stage]).real:
            here += 1
        if use == name:
            return n + here
    raise KeyError(name)


def ma_count(batch, name):
    return batch.count(len(MA_FILLS), MA_FILLS.index(name) + 1)


def steps(eng):
    for it in range(-2, 2):
        yield Batch(it)
    with eng.Fori(0, 2) as r:
        yield Batch(2, r)
        yield Batch(3, r)
    for it in range(6, B + 1):
        yield Batch(it)


def layer_kernel(nc, x, xT, wqkv, wo, wg, wu, wd, ident, cos, sin, out):
    nc.disable_value_cache = True
    with ExitStack() as ctx:
        def sb(name, shape, dt=F32):
            return ctx.enter_context(nc.sbuf_tensor(name, shape, dt))

        def ps(name, shape, dt=F32):
            return ctx.enter_context(nc.psum_tensor(name, shape, dt))

        def sem(name):
            return ctx.enter_context(nc.semaphore(name))

        wqkv_sb = sb("wqkv_sb", [P, KC, QKV])
        wo_sb = sb("wo_sb", [P, KC, D])
        wg_sb = sb("wg_sb", [P, KC, 8, P])
        wu_sb = sb("wu_sb", [P, KC, 8, P])
        wd_sb = sb("wd_sb", [P, 8, D])
        id_f = sb("id_f", [P, P])
        id_b = sb("id_b", [P, P], BF16)
        cos_sb = sb("cos_sb", [P, TT, HD])
        sin_sb = sb("sin_sb", [P, TT, HD])
        half_neg = sb("half_neg", [P, 2])
        xT_sb = sb("xT_sb", [P, KC, S])
        qk_sb = sb("qk_sb", [P, TT, QK])
        v_raw = sb("v_raw", [P, TT, KV * HD])
        rot_s = sb("rot_s", [P, TT, P])
        part = sb("part", [P, PARTS, TT, QK], BF16)
        part_T = sb("part_T", [P, len(PT_ORDER), S], BF16)
        q_stack = [sb(f"q_stack{n}", [P, H, S], BF16) for n in range(2)]
        k_stack = [sb(f"k_stack{n}", [P, KV, S], BF16) for n in range(2)]
        v_aug = [sb(f"v_aug{n}", [P, TT, KV, 32]) for n in range(2)]
        row_max = sb("row_max", [P, 2, TT, H // 2])
        max_rest = sb("max_rest", [P, TT, H // 2])
        neg_part = sb("neg_part", [P, TT, PARTS, H // 2], BF16)
        neg_T = sb("neg_T", [PARTS * H // 2, 2, S], BF16)
        prob = sb("prob", [P, 8, S])
        oT_sb = sb("oT_sb", [P, S])
        recip = sb("recip", [P, TT, 4])
        o_sb = sb("o_sb", [P, TT, D])
        feat_T = sb("feat_T", [P, KC, S])
        xr = sb("xr", [P, TT, D])
        stats = sb("stats", [P, TT, 6])
        mv = sb("mv", [P, TT, 2])
        var_eps = sb("var_eps", [P, TT])
        rstd = sb("rstd", [P, TT])
        th = sb("th", [P, D])
        gate = sb("gate", [P, D])
        hid = sb("hid", [P, 8, S])
        mag = sb("mag", [P, 4, 256])
        beats = sb("beats", [P, 6, 256], BF16)
        wins = sb("wins", [P, 4, 256], BF16)

        ps_m = ps("ps_m", [P, 2, 512])
        ps_s = ps("ps_s", [P, SB, 512])
        ps_o = ps("ps_o", [P, 512])
        ma = ps("ma", [P, 512])
        mb = ps("mb", [P, 512])
        mb_b = mb[:, :].bitcast(BF16)

        weights_in = sem("weights_in")
        consts_set = sem("consts_set")
        id_ready = sem("id_ready")
        xT_in = sem("xT_in")
        x_in = sem("x_in")
        ma_filled, ma_read = sem("ma_filled"), sem("ma_read")
        mb_filled, mb_read = sem("mb_filled"), sem("mb_read")
        v_built = sem("v_built")
        parts_made = sem("parts_made")
        stack_lo, stack_hi = sem("stack_lo"), sem("stack_hi")
        scored = sem("scored")
        maxed = sem("maxed")
        neg_made = sem("neg_made")
        aug_lo, aug_hi = sem("aug_lo"), sem("aug_hi")
        st_ready = sem("st_ready")
        exp_done = sem("exp_done")
        pv_done = sem("pv_done")
        oT_copied = sem("oT_copied")
        recip_made = sem("recip_made")
        summed = sem("summed")
        stat_made = sem("stat_made")
        var_made = sem("var_made")
        rstd_made = sem("rstd_made")
        ln_done = sem("ln_done")
        tanh_done = sem("tanh_done")
        gate_made = sem("gate_made")
        mag_made = sem("mag_made")
        compared = sem("compared")
        wins_made = sem("wins_made")
        sparse_made = sem("sparse_made")
        rot_step = sem("rot_step")
        neg_step = sem("neg_step")
        wins_step = sem("wins_step")
        v_zeroed = sem("v_zeroed")
        passed = sem("passed")
        out_done = sem("out_done")

        block = ctx.enter_context(nc.Block())

        @block.sync
        def _(sp):
            for dst, src in ((wqkv_sb, wqkv), (id_f, ident), (cos_sb, cos), (sin_sb, sin),
                             (wo_sb, wo), (wg_sb, wg), (wu_sb, wu), (wd_sb, wd)):
                sp.dma_start(dst[:], src).then_inc(weights_in, 16)

            def scatter(b, chunk, half, done):
                par = b.parity
                for i in range(PARTS):
                    for j in range(PARTS):
                        row = 24 * i + 8 * j
                        src = part_T[:, PT_ORDER.index((i, chunk)), :]
                        sp.dma_start(q_stack[par][row:row + 8, 16 * half:16 * half + 16, :],
                                     src).then_inc(done, 16)
                        src = part_T[32 * half:32 * half + 32, PT_ORDER.index((j, 2)), :]
                        sp.dma_start(k_stack[par][row:row + 8, 4 * half:4 * half + 4, :],
                                     src).then_inc(done, 16)

            for step in steps(sp):
                bA, bM, bB, bF = (step.plus(LAG[s]) for s in "AMBF")
                if bA.real:
                    if bA.r is not None or bA.first > 0:
                        sp.wait_ge(mb_filled, mb_count(step.plus(-1), "qkv3"))
                    sp.dma_start(xT_sb[:], xT[bA.index]).then_inc(xT_in, 16)
                if bF.real:
                    sp.wait_ge(out_done, bF.count(32, 0))
                    sp.dma_start(xr[:], x[bF.index].rearrange("(t p) d -> p t d", p=P)).then_inc(x_in, 16)
                if bM.real:
                    sp.wait_ge(mb_read, mb_count(step.plus(-1), "pT4"))
                    sp.wait_ge(pv_done, bM.plus(-2).count(32, 32))
                    if bM.first < 2 and bM.r is None:
                        sp.wait_ge(consts_set, 2)
                    scatter(bM, 1, 1, stack_hi)
                if bB.real:
                    sp.wait_ge(mb_read, mb_count(step, "mt1"))
                    sp.dma_start(q_stack[bB.parity][AUG:AUG + 3, 16:32, :], neg_T[:, 1, :]).then_inc(aug_hi, 16)
                if bA.real:
                    sp.wait_ge(mb_read, mb_count(step, "pT2"))
                    sp.wait_ge(pv_done, bA.plus(-2).count(32, 16))
                    if bA.first < 2 and bA.r is None:
                        sp.wait_ge(consts_set, 2)
                    scatter(bA, 0, 0, stack_lo)
                if bM.real:
                    sp.wait_ge(mb_read, mb_count(step, "mt0"))
                    sp.dma_start(q_stack[bM.parity][AUG:AUG + 3, 0:16, :], neg_T[:, 0, :]).then_inc(aug_lo, 16)
                if bF.real:
                    for half in range(2):
                        sp.wait_ge(ln_done, bF.count(8, 4 + 2 * half + 2))
                        dst = out[bF.index].rearrange("(t p) d -> p t d", p=P)
                        sp.dma_start(dst[:, 2 * half:2 * half + 2, :],
                                     xr[:, 2 * half:2 * half + 2, :]).then_inc(out_done, 16)
            sp.wait_ge(out_done, 32 * B)

        @block.tensor
        def _(pe):
            pe.wait_ge(weights_in, 16 * 8)
            pe.wait_ge(consts_set, 2)

            def max_scores(step, slot, qt):
                b = step.plus(LAG["M"])
                n = 4 * slot + qt
                if slot == 0 and qt == 0:
                    pe.wait_ge(stack_lo, b.count(288, 288))
                if slot == 16 and qt == 0:
                    pe.wait_ge(stack_hi, b.count(288, 288))
                pe.wait_ge(maxed, b.count(128, n - 1))
                nc.tensor.matmul(ps_m[:, n % 2, :], q_stack[b.parity][0:AUG, slot, qt * P:(qt + 1) * P],
                                 k_stack[b.parity][0:AUG, slot // 4, :], start=True, stop=True).then_inc(scored, 1)

            def key_scores(step, slot, i):
                b = step.plus(LAG["B"])
                g, kt = slot // 4, slot % 4
                n = 4 * slot + i
                if slot == 0 and i == 0:
                    pe.wait_ge(aug_lo, b.count(16, 16))
                if slot == 16 and i == 0:
                    pe.wait_ge(aug_hi, b.count(16, 16))
                free = n - 2 if n >= SB else (-1, 0, -2)[n]
                pe.wait_ge(exp_done, b.count(128, free))
                nc.tensor.matmul(ps_s[:, n % SB, :], k_stack[b.parity][:, g, kt * P:(kt + 1) * P],
                                 q_stack[b.parity][:, 4 * g + i, :], start=True, stop=True).then_inc(st_ready, 1)

            def values(step, quad):
                b = step.plus(LAG["B"])
                g, kt = quad // 4, quad % 4
                if quad == 0:
                    pe.wait_ge(v_built, b.count(1, 1))
                if kt == 0:
                    pe.wait_ge(oT_copied, b.count(8, g))
                pe.wait_ge(exp_done, b.count(128, 4 * quad + 4))
                for i in range(4):
                    mm = nc.tensor.matmul(ps_o[32 * i:32 * i + 32, :], v_aug[b.parity][:, kt, g, :],
                                          prob[:, (4 * quad + i) % 8, :], start=(kt == 0), stop=(kt == 3))
                mm.then_inc(pv_done, 1)

            def side_mb(step, name, b):
                pe.wait_ge(mb_read, mb_count(step, name) - 1)
                if name.startswith("ott"):
                    g = int(name[3:])
                    pe.wait_ge(oT_copied, b.count(8, g + 1))
                    for qt in range(TT):
                        mm = nc.tensor.transpose(mb[:, qt * P:(qt + 1) * P], oT_sb[:, qt * P:(qt + 1) * P], id_f[:])
                elif name.startswith("oT"):
                    kc = int(name[2:])
                    pe.wait_ge(mb_read, mb_count(step, "ott7"))
                    for tt in range(TT):
                        mm = nc.tensor.transpose(mb[:, tt * P:(tt + 1) * P], o_sb[:, tt, kc * P:(kc + 1) * P], id_f[:])
                elif name.startswith("xT"):
                    kc = int(name[2:])
                    pe.wait_ge(ln_done, b.count(8, 4))
                    for tt in range(TT):
                        mm = nc.tensor.transpose(mb[:, tt * P:(tt + 1) * P], xr[:, tt, kc * P:(kc + 1) * P], id_f[:])
                elif name.startswith("qkv"):
                    tt = int(name[3:])
                    pe.wait_ge(xT_in, b.count(16, 16))
                    for kc in range(KC):
                        mm = nc.tensor.matmul(mb[:, 0:QKV], xT_sb[:, kc, tt * P:(tt + 1) * P], wqkv_sb[:, kc, :],
                                              start=(kc == 0), stop=(kc == KC - 1))
                elif name.startswith("pT"):
                    u = int(name[2:])
                    pe.wait_ge(parts_made, b.count(1, 1))
                    pe.sem_inc(passed, 1)
                    for k, (i, c) in enumerate(PT_ORDER[2 * u:2 * u + 2]):
                        w = P if c < 2 else KV * HD
                        for tt in range(TT):
                            mm = nc.tensor.transpose(mb_b[0:w, k * S + tt * P:k * S + (tt + 1) * P],
                                                     part[:, i, tt, c * P:c * P + w], id_b[:])
                else:
                    half = int(name[2:])
                    pe.wait_ge(neg_made, b.count(2, half + 1))
                    pe.sem_inc(passed, 1)
                    for qt in range(TT):
                        mm = nc.tensor.transpose(mb_b[0:PARTS * H // 2, qt * P:(qt + 1) * P],
                                                 neg_part[:, qt, :, :].rearrange("p a h -> p (a h)"), id_b[:])
                mm.then_inc(mb_filled, 1)

            def side_ma(step, name, b):
                if name in MA_FILLS and name not in ("dn1", "dn3"):
                    pe.wait_ge(ma_read, ma_count(b, name) - 1)
                if name.startswith("wo"):
                    pe.wait_ge(mb_read, mb_count(step, "oT1"))
                    for k in range(2):
                        tt = 2 * int(name[2:]) + k
                        for kc in range(KC):
                            mm = nc.tensor.matmul(ma[:, k * D:(k + 1) * D], feat_T[:, kc, tt * P:(tt + 1) * P],
                                                  wo_sb[:, kc, :], start=(kc == 0), stop=(kc == KC - 1))
                    mm.then_inc(ma_filled, 1)
                elif name.startswith("gu"):
                    f = int(name[2:])
                    u, j = f // 4, f % 4
                    half, t = u // 2, u % 2
                    if f == 0:
                        pe.wait_ge(mb_read, mb_count(step, "xT1"))
                    for k, w in enumerate((wg_sb, wu_sb)):
                        for kc in range(KC):
                            mm = nc.tensor.matmul(ma[:, k * 256:(k + 1) * 256], w[:, kc, 4 * t + j, :],
                                                  feat_T[:, kc, half * 256:(half + 1) * 256],
                                                  start=(kc == 0), stop=(kc == KC - 1))
                    mm.then_inc(ma_filled, 1)
                else:
                    tt = int(name[2:])
                    if tt % 2 == 0:
                        pe.wait_ge(sparse_made, b.count(4, tt + 2))
                        pe.wait_ge(ma_read, ma_count(b, f"dn{tt + 1}") - 1)
                    for n in range(8):
                        mm = nc.tensor.matmul(ma[:, (tt % 2) * D:(tt % 2 + 1) * D], hid[:, n, tt * P:(tt + 1) * P],
                                              wd_sb[:, n, :], start=(n == 0), stop=(n == 7))
                    if tt % 2 == 1:
                        mm.then_inc(ma_filled, 1)

            def side(step, slot, half):
                for at, name, stage in MB_USES:
                    b = step.plus(LAG[stage])
                    if at == (slot, half) and b.real:
                        side_mb(step, name, b)
                for at, name in MA_USES:
                    b = step.plus(LAG["F"])
                    if at == (slot, half) and b.real:
                        side_ma(step, name, b)

            for step in steps(pe):
                has_m, has_b = step.plus(1).real, step.real
                for slot in range(SLOTS):
                    for half in range(2):
                        for i in (2 * half, 2 * half + 1):
                            if has_b:
                                key_scores(step, slot, i)
                            if has_m:
                                max_scores(step, slot, i)
                        side(step, slot, half)
                    if has_b and slot >= 1:
                        values(step, slot - 1)
                if has_b:
                    values(step, SLOTS - 1)

        @block.scalar
        def _(act):
            def exps(step, slot, i):
                b = step.plus(LAG["B"])
                n = 4 * slot + i
                if i == 0:
                    act.wait_ge(pv_done, b.count(32, slot - 1))
                act.wait_ge(st_ready, b.count(128, n + 1))
                nc.scalar.activation(prob[:, n % 8, :], ps_s[:, n % SB, :], ACT.Exp, scale=SCALE).then_inc(exp_done, 1)

            def output_copy(b, g, last_use):
                act.wait_ge(pv_done, b.count(32, 4 * g + 4))
                if last_use is not None:
                    act.wait_ge(mb_filled, last_use)
                nc.scalar.copy(oT_sb[:], ps_o[:]).then_inc(oT_copied, 1)

            def side(step, slot, half):
                for at, name, stage in MB_USES:
                    b = step.plus(LAG[stage])
                    if at != (slot, half) or not b.real or name.startswith("ott"):
                        continue
                    act.wait_ge(mb_filled, mb_count(step, name))
                    if name.startswith("qkv"):
                        tt = int(name[3:])
                        if tt == 0:
                            act.wait_ge(parts_made, b.count(1, 0))
                            act.wait_ge(v_built, b.count(1, 0))
                        nc.scalar.copy(v_raw[:, tt, :], mb[:, QK:QKV])
                        nc.scalar.copy(qk_sb[:, tt, :], mb[:, 0:QK]).then_inc(mb_read, 1)
                    elif name.startswith("pT"):
                        u = int(name[2:])
                        if u == 0:
                            act.wait_ge(stack_lo, b.count(288, 0))
                            act.wait_ge(stack_hi, b.count(288, 0))
                        chunks = PT_ORDER[2 * u:2 * u + 2]
                        if len({c < 2 for _, c in chunks}) == 1:
                            w = P if chunks[0][1] < 2 else KV * HD
                            cp = nc.scalar.copy(part_T[0:w, 2 * u:2 * u + len(chunks), :],
                                                mb_b[0:w, 0:len(chunks) * S].rearrange("p (k t) -> p k t", t=S))
                            cp.then_inc(mb_read, 1)
                        else:
                            nc.scalar.copy(part_T[0:P, 2 * u, :], mb_b[0:P, 0:S])
                            nc.scalar.copy(part_T[0:KV * HD, 2 * u + 1, :], mb_b[0:KV * HD, S:2 * S]).then_inc(mb_read, 1)
                    elif name.startswith("mt"):
                        half_of = int(name[2:])
                        act.wait_ge(aug_hi if half_of else aug_lo, b.count(16, 0))
                        n = PARTS * H // 2
                        nc.scalar.copy(neg_T[:, half_of, :], mb_b[0:n, 0:S]).then_inc(mb_read, 1)
                    else:
                        kc = int(name[2:])
                        if name.startswith("xT"):
                            act.wait_ge(ma_filled, ma_count(b, "wo1"))
                        nc.scalar.copy(feat_T[:, kc, :], mb[:, :]).then_inc(mb_read, 1)
                for at, name in MA_USES:
                    b = step.plus(LAG["F"])
                    if at == (slot, half) and b.real and name.startswith("gu"):
                        act.wait_ge(ma_filled, ma_count(b, name))
                        nc.scalar.activation(th[:], ma[:, 0:256], ACT.Tanh, scale=0.5).then_inc(tanh_done, 1)

            for step in steps(act):
                bB, bF = step.plus(LAG["B"]), step.plus(LAG["F"])
                for slot in range(SLOTS):
                    if slot == 1 and bF.real:
                        output_copy(bF, 7, mb_count(step.plus(-1), "ott6"))
                    if slot % 4 == 1 and slot >= 5 and bB.real:
                        g = slot // 4 - 1
                        prev = f"ott{g - 1}" if g else "ott7"
                        output_copy(bB, g, mb_count(step, prev) if g or bF.real else None)
                    if slot in (15, 17, 19, 21) and bF.real:
                        u = (slot - 15) // 2
                        act.wait_ge(ma_read, ma_count(bF, f"gu{4 * u + 3}"))
                        act.wait_ge(compared, bF.count(4, u))
                        nc.scalar.activation(mag[:], hid[:, 4 * (u % 2):4 * (u % 2) + 4, 256 * (u // 2):256 * (u // 2) + 256],
                                             ACT.Abs).then_inc(mag_made, 1)
                    for half in range(2):
                        if bB.real:
                            exps(step, slot, 2 * half)
                            exps(step, slot, 2 * half + 1)
                        side(step, slot, half)

        @block.vector
        def _(dve):
            nc.vector.memset(k_stack[0][:].bitcast(F32), 0.0).then_inc(id_ready, 1)
            nc.vector.memset(k_stack[1][:].bitcast(F32), 0.0).then_inc(id_ready, 1)
            nc.vector.memset(q_stack[0][:].bitcast(F32), 0.0)
            dve.wait_ge(id_ready, 2)
            nc.vector.memset(k_stack[0][AUG:AUG + 3, :, :], 1.0)
            nc.vector.memset(k_stack[1][AUG:AUG + 3, :, :], 1.0)
            dve.wait_ge(weights_in, 16 * 8)
            nc.vector.tensor_copy(id_b[:], id_f[:]).then_inc(consts_set, 1)

            def row_maximum(step, slot, qt):
                b = step.plus(LAG["M"])
                n = 4 * slot + qt
                if n == 0:
                    dve.wait_ge(neg_made, b.count(2, -1))
                if n == 64:
                    dve.wait_ge(neg_made, b.count(2, 0))
                dve.wait_ge(scored, b.count(128, n + 1))
                nc.vector.tensor_reduce(row_max[:, slot // 16, qt, slot % 16:slot % 16 + 1], ps_m[:, n % 2, :],
                                        AX.X, ALU.max).then_inc(maxed, 1)

            def normalise_group(step, b, name):
                g = int(name[3:])
                dve.wait_ge(mb_filled, mb_count(step, name))
                t = mb[:, :].rearrange("p (t i c) -> p t i c", t=TT, i=4)
                nc.vector.reciprocal(recip[:], t[:, :, :, HD]).then_inc(recip_made, 1)
                dve.wait_ge(recip_made, b.count(8, g + 1))
                nc.vector.tensor_tensor(o_sb[:, :, 32 * g:32 * g + 32].rearrange("p t (i d) -> p t i d", i=4),
                                        t[:, :, :, 0:HD], recip[:].unsqueeze(3).broadcast_to([P, TT, 4, HD]),
                                        ALU.mult).then_inc(mb_read, 1)

            def residual(b, which, half, name):
                dve.wait_ge(ma_filled, ma_count(b, name))
                sl = xr[:, 2 * half:2 * half + 2, :]
                nc.vector.tensor_tensor(sl, ma[:, :].rearrange("p (k d) -> p k d", k=2), sl, ALU.add).then_inc(ma_read, 1)
                dve.wait_ge(ma_read, ma_count(b, name))
                for k in range(2):
                    tt = 2 * half + k
                    nc.vector.bn_stats(stats[:, tt, :], xr[:, tt, :]).then_inc(summed, 1)
                    dve.wait_ge(summed, b.count(8, 4 * which + tt + 1))
                    dve.sem_inc(passed, 1)
                    nc.vector.bn_aggr(mv[:, tt, :], stats[:, tt, :]).then_inc(stat_made, 1)

            def normalise(b, which, tiles):
                for tt in tiles:
                    dve.wait_ge(rstd_made, b.count(4, 2 * which + tt // 2 + 1))
                    nc.vector.tensor_scalar(xr[:, tt, :], xr[:, tt, :], mv[:, tt, 0:1], rstd[:, tt:tt + 1],
                                            ALU.subtract, ALU.mult).then_inc(ln_done, 1)

            def swiglu(b, f):
                u, j = f // 4, f % 4
                half, t = u // 2, u % 2
                dve.wait_ge(tanh_done, b.count(16, f + 1))
                nc.vector.scalar_tensor_tensor(out=gate[:], in0=th[:], scalar=1.0, in1=ma[:, 0:256],
                                               op0=ALU.add, op1=ALU.mult).then_inc(gate_made, 1)
                dve.wait_ge(gate_made, b.count(16, f + 1))
                nc.vector.scalar_tensor_tensor(out=hid[:, 4 * t + j, half * 256:(half + 1) * 256], in0=gate[:],
                                               scalar=0.5, in1=ma[:, 256:512], op0=ALU.mult,
                                               op1=ALU.mult).then_inc(ma_read, 1)

            def compare(b, u):
                dve.wait_ge(mag_made, b.count(4, u + 1))
                dve.wait_ge(wins_made, b.count(4, u))
                nc.vector.tensor_tensor(beats[:, 0:2, :], mag[:, 0:4:2, :], mag[:, 1:4:2, :], ALU.is_ge)
                nc.vector.tensor_tensor(beats[:, 2:4, :], mag[:, 0:2, :], mag[:, 2:4, :], ALU.is_ge)
                nc.vector.tensor_tensor(beats[:, 4, :], mag[:, 0, :], mag[:, 3, :], ALU.is_ge)
                nc.vector.tensor_tensor(beats[:, 5, :], mag[:, 1, :], mag[:, 2, :], ALU.is_ge).then_inc(compared, 1)

            def sparsify(b, u):
                dve.wait_ge(wins_made, b.count(4, u + 1))
                half, t = u // 2, u % 2
                for j, (op, bound) in enumerate(((ALU.is_ge, 2.0), (ALU.is_ge, 1.0), (ALU.is_ge, 0.0), (ALU.is_le, 1.0))):
                    h = hid[:, 4 * t + j, half * 256:(half + 1) * 256]
                    last = nc.vector.scalar_tensor_tensor(out=h, in0=wins[:, j, :], scalar=bound, in1=h,
                                                          op0=op, op1=ALU.mult)
                last.then_inc(sparse_made, 1)

            for step in steps(dve):
                bM, bB, bF = (step.plus(LAG[s]) for s in "MBF")
                for slot in range(SLOTS):
                    if bF.real:
                        if slot == 10:
                            normalise(bF, 0, range(TT))
                        if slot in (16, 18, 20, 22):
                            compare(bF, (slot - 16) // 2)
                        if slot in (19, 21, 23, 25):
                            sparsify(bF, (slot - 19) // 2)
                        if slot == 26:
                            normalise(bF, 1, (0, 1))
                        if slot == 30:
                            normalise(bF, 1, (2, 3))
                    for half in range(2):
                        if bM.real:
                            row_maximum(step, slot, 2 * half)
                            row_maximum(step, slot, 2 * half + 1)
                        for at, name, stage in MB_USES:
                            b = step.plus(LAG[stage])
                            if at == (slot, half) and b.real and name.startswith("ott"):
                                if name == "ott0" and bF.real:
                                    dve.wait_ge(mb_filled, mb_count(step, "oT1"))
                                normalise_group(step, b, name)
                        for at, name in MA_USES:
                            if at == (slot, half) and bF.real:
                                if name.startswith("wo"):
                                    if name == "wo0":
                                        dve.wait_ge(x_in, bF.count(16, 16))
                                    residual(bF, 0, int(name[2:]), name)
                                elif name.startswith("gu"):
                                    swiglu(bF, int(name[2:]))
                                elif name in ("dn1", "dn3"):
                                    residual(bF, 1, int(name[2:]) // 2, name)

        @block.gpsimd
        def _(pool):
            for n in range(2):
                nc.gpsimd.memset(v_aug[n][:], 0.0).then_inc(v_zeroed, 1)
            nc.gpsimd.memset(q_stack[1][:].bitcast(F32), 0.0)
            nc.gpsimd.memset(half_neg[:], -0.5)
            pool.wait_ge(v_zeroed, 2)
            nc.gpsimd.memset(v_aug[0][:, :, :, HD:HD + 1], 1.0)
            nc.gpsimd.memset(v_aug[1][:, :, :, HD:HD + 1], 1.0).then_inc(consts_set, 1)
            pool.wait_ge(consts_set, 2)
            pool.wait_ge(weights_in, 16 * 8)

            def build_v(step, b):
                pool.wait_ge(mb_read, mb_count(step.plus(-1), "qkv3"))
                pool.wait_ge(pv_done, b.plus(-2).count(32, 32))
                pool.sem_inc(passed, 1)
                nc.gpsimd.tensor_copy(v_aug[b.parity][:, :, :, 0:HD],
                                      v_raw[:].rearrange("p t (k d) -> p t k d", d=HD)).then_inc(v_built, 1)

            def split_negated(b, half, last_transposed):
                m = row_max[:, half]
                if last_transposed is not None:
                    pool.wait_ge(mb_filled, last_transposed)
                pool.wait_ge(maxed, b.count(128, 64 * (half + 1)))
                pool.sem_inc(passed, 1)
                k = 4 * half
                nc.gpsimd.tensor_scalar(neg_part[:, :, 0, :], m, -1.0, None, ALU.mult).then_inc(neg_step, 1)
                pool.wait_ge(neg_step, b.count(8, k + 1))
                nc.gpsimd.tensor_tensor(max_rest[:], m, neg_part[:, :, 0, :], ALU.add).then_inc(neg_step, 1)
                pool.wait_ge(neg_step, b.count(8, k + 2))
                pool.sem_inc(passed, 1)
                nc.gpsimd.tensor_scalar(neg_part[:, :, 1, :], max_rest[:], -1.0, None, ALU.mult).then_inc(neg_step, 1)
                pool.wait_ge(neg_step, b.count(8, k + 3))
                nc.gpsimd.tensor_tensor(max_rest[:], max_rest[:], neg_part[:, :, 1, :], ALU.add).then_inc(neg_step, 1)
                pool.wait_ge(neg_step, b.count(8, k + 4))
                pool.sem_inc(passed, 1)
                nc.gpsimd.tensor_scalar(neg_part[:, :, 2, :], max_rest[:], -1.0, None, ALU.mult).then_inc(neg_made, 1)

            def inverse_std(b, which, half):
                k = 2 * which + half + 1
                pool.wait_ge(stat_made, b.count(8, 2 * k))
                pool.sem_inc(passed, 1)
                sl = slice(2 * half, 2 * half + 2)
                nc.gpsimd.tensor_scalar(var_eps[:, sl], mv[:, sl, 1], EPS, None, ALU.add).then_inc(var_made, 1)
                pool.wait_ge(var_made, b.count(4, k))
                nc.gpsimd.tensor_tensor(rstd[:, sl], var_eps[:, sl], half_neg[:], ALU.pow).then_inc(rstd_made, 1)

            def rotate_and_split(step, b):
                pool.wait_ge(mb_read, mb_count(step, "qkv3"))
                if not (b.r is None and b.first == 0):
                    pool.wait_ge(mb_filled, mb_count(step.plus(-1), "pT4"))
                n = 0
                for off, w in ((0, P), (P, P), (2 * P, 32), (2 * P + 32, 32)):
                    q = qk_sb[:, :, off:off + w].rearrange("p t (d h) -> p t d h", d=HD)
                    heads = w // HD
                    s = rot_s[:, :, 0:w].rearrange("p t (d h) -> p t d h", d=HD)
                    c_ = cos_sb[:].unsqueeze(3).broadcast_to([P, TT, HD, heads])
                    s_ = sin_sb[:].unsqueeze(3).broadcast_to([P, TT, HD, heads])
                    nc.gpsimd.tensor_tensor(s[:, :, 0:4], q[:, :, 4:8], s_[:, :, 0:4], ALU.mult)
                    nc.gpsimd.tensor_tensor(s[:, :, 4:8], q[:, :, 0:4], s_[:, :, 4:8], ALU.mult).then_inc(rot_step, 1)
                    n += 1
                    pool.wait_ge(rot_step, b.count(16, n))
                    nc.gpsimd.tensor_tensor(q, q, c_, ALU.mult).then_inc(rot_step, 1)
                    n += 1
                    pool.wait_ge(rot_step, b.count(16, n))
                    nc.gpsimd.tensor_tensor(q, q, s, ALU.add).then_inc(rot_step, 1)
                    n += 1
                    if n < 12:
                        pool.wait_ge(rot_step, b.count(16, n))
                pool.wait_ge(rot_step, b.count(16, n))
                pool.sem_inc(passed, 1)
                for i in range(PARTS):
                    cast = nc.gpsimd.tensor_copy(part[:, i], qk_sb[:])
                    if i == PARTS - 1:
                        cast.then_inc(parts_made, 1)
                        break
                    cast.then_inc(rot_step, 1)
                    n += 1
                    pool.wait_ge(rot_step, b.count(16, n))
                    nc.gpsimd.tensor_tensor(qk_sb[:], qk_sb[:], part[:, i], ALU.subtract).then_inc(rot_step, 1)
                    n += 1
                    pool.wait_ge(rot_step, b.count(16, n))
                    pool.sem_inc(passed, 1)
                assert n == 16

            def count_wins(b, u):
                pool.wait_ge(compared, b.count(4, u + 1))
                pool.wait_ge(sparse_made, b.count(4, u))
                m01, m23, m02, m13, m03, m12 = (beats[:, k, :] for k in range(6))
                nc.gpsimd.tensor_tensor(wins[:, 0, :], m02, m03, ALU.add)
                nc.gpsimd.tensor_tensor(wins[:, 1, :], m13, m12, ALU.add)
                nc.gpsimd.tensor_tensor(wins[:, 2, :], m02, m12, ALU.add)
                nc.gpsimd.tensor_tensor(wins[:, 3, :], m03, m13, ALU.add).then_inc(wins_step, 1)
                pool.wait_ge(wins_step, b.count(4, u + 1))
                nc.gpsimd.tensor_tensor(wins[:, 0, :], wins[:, 0, :], m01, ALU.add)
                nc.gpsimd.tensor_tensor(wins[:, 1, :], wins[:, 1, :], m01, ALU.subtract)
                nc.gpsimd.tensor_tensor(wins[:, 2, :], m23, wins[:, 2, :], ALU.subtract)
                nc.gpsimd.tensor_tensor(wins[:, 3, :], wins[:, 3, :], m23, ALU.add).then_inc(wins_made, 1)

            for step in steps(pool):
                bA, bM, bB, bF = (step.plus(LAG[s]) for s in "AMBF")
                if bM.real:
                    build_v(step, bM)
                if bB.real:
                    split_negated(bB, 1, mb_count(step.plus(-1), "mt0"))
                if bF.real:
                    inverse_std(bF, 0, 0)
                    inverse_std(bF, 0, 1)
                if bA.real:
                    rotate_and_split(step, bA)
                if bF.real:
                    count_wins(bF, 0)
                if bM.real:
                    split_negated(bM, 0, mb_count(step, "mt1") if bB.real else None)
                if bF.real:
                    for u in range(1, 4):
                        count_wins(bF, u)
                    inverse_std(bF, 1, 0)
                    inverse_std(bF, 1, 1)


def kernel(L0_attn_x, L0_attn_Wq, L0_attn_Wk, L0_attn_Wv, L0_attn_Wo, L0_ffn_w_gate, L0_ffn_w_up, L0_ffn_w_down):
    import concourse.bacc as _bacc
    from concourse.bass_utils import run_bass_kernel_spmd as _run

    x = np.asarray(L0_attn_x)
    wq = np.asarray(L0_attn_Wq).reshape(2, H // 2, HD, D).transpose(0, 2, 1, 3).reshape(H * HD, D)
    wk = np.asarray(L0_attn_Wk).reshape(2, KV // 2, HD, D).transpose(0, 2, 1, 3).reshape(KV * HD, D)
    wqkv = np.concatenate([wq, wk, np.asarray(L0_attn_Wv)], axis=0)

    def chunks(w):
        return w.reshape(KC, P, -1).transpose(1, 0, 2)

    def hidden_tiles(w):
        return w.reshape(KC, P, 2, P, 4).transpose(1, 0, 2, 4, 3).reshape(P, KC, 8, P)

    inv = (1.0 / np.float32(10000.0) ** (np.arange(0, HD, 2, dtype=np.float32) / HD)).astype(np.float32)
    ang = np.arange(S, dtype=np.float32)[:, None] * inv[None, :]
    cos = np.concatenate([np.cos(ang), np.cos(ang)], axis=1).reshape(TT, P, HD).transpose(1, 0, 2)
    sin = np.concatenate([-np.sin(ang), np.sin(ang)], axis=1).reshape(TT, P, HD).transpose(1, 0, 2)
    data = {
        "x": x,
        "xT": x.reshape(B, S, KC, P).transpose(0, 3, 2, 1),
        "wqkv": chunks(wqkv.T),
        "wo": chunks(np.asarray(L0_attn_Wo).T),
        "wg": hidden_tiles(np.asarray(L0_ffn_w_gate)),
        "wu": hidden_tiles(np.asarray(L0_ffn_w_up)),
        "wd": np.asarray(L0_ffn_w_down).reshape(2, P, 4, D).transpose(1, 0, 2, 3).reshape(P, 8, D),
        "ident": np.eye(P, dtype=np.float32),
        "cos": cos, "sin": sin,
    }
    nc = _bacc.Bacc("TRN2", target_bir_lowering=False, num_devices=1)
    arrays, args = {}, []
    for name, a in data.items():
        a = np.ascontiguousarray(a)
        arrays[f"in_{name}"] = a
        args.append(nc.dram_tensor(f"in_{name}", a.shape, mybir.dt.from_np(a.dtype), kind="ExternalInput").ap())
    args.append(nc.dram_tensor("out_0", (B, S, D), F32, kind="ExternalOutput").ap())
    layer_kernel(nc, *args)
    return _run(nc, [arrays], core_ids=[0]).results[0]["out_0"]
```

```python
from contextlib import ExitStack

import numpy as np

import concourse.bass as bass
from concourse import mybir

F32 = mybir.dt.float32
BF16 = mybir.dt.bfloat16
ALU = mybir.AluOpType
ACT = mybir.ActivationFunctionType
AX = mybir.AxisListType

P = 128
B, S, D = 8, 512, 256
H, KV, HD = 32, 8, 8
I = 1024
TT = S // P
KC = D // P
QK = (H + KV) * HD
QKV = QK + KV * HD
GROUPS = H // 4
SLOTS = H
PARTS = 3
AUG = 96
SCALE = HD ** -0.5
EPS = 1e-5
LEAD = 20

MB_USES = [
    ((0, 1), "qkv0", "A"), ((1, 1), "qkv1", "A"), ((1, 2), "ott7", "F"), ((2, 1), "oT0", "F"),
    ((2, 3), "oT1", "F"), ((3, 3), "qkv2", "A"), ((5, 1), "qkv3", "A"), ((6, 0), "ott0", "B"),
    ((6, 1), "xT0", "F"), ((6, 3), "xT1", "F"), ((10, 0), "ott1", "B"), ((13, 2), "mt1", "B"),
    ((14, 0), "ott2", "B"), ((14, 2), "pT0", "A"), ((15, 2), "pT1", "A"), ((17, 2), "pT2", "A"),
    ((18, 0), "ott3", "B"), ((19, 2), "pT3", "A"), ((21, 2), "pT4", "A"), ((22, 0), "ott4", "B"),
    ((26, 0), "ott5", "B"), ((29, 2), "mt0", "M"), ((30, 0), "ott6", "B"),
]
WO_SLOT, GU_SLOT, DN_SLOT = 3, 7, 23
MA_FILLS = ["wo0", "wo1"] + [f"gu{f}" for f in range(16)] + ["dn0", "dn1"]
PT_ORDER = [(0, 0), (1, 0), (2, 0), (0, 2), (1, 2), (2, 2), (0, 1), (1, 1), (2, 1)]
LAG = {"A": 2, "M": 1, "B": 0, "F": -1, "E": -2}


class Batch:

    def __init__(self, first, r=None, stride=2):
        self.first, self.r, self.stride = first, r, stride

    def plus(self, n):
        return Batch(self.first + n, self.r, self.stride)

    @property
    def real(self):
        return self.r is not None or 0 <= self.first < B

    @property
    def parity(self):
        return self.first % 2

    def count(self, per, more):
        v = self.first * per + more
        return max(v, 0) if self.r is None else v + self.r * (self.stride * per)

    @property
    def index(self):
        return self.count(1, 0)


def mb_count(step, name):
    n = 0
    for stage in "AMBF":
        per = sum(1 for _, _, s in MB_USES if s == stage)
        b = step.plus(LAG[stage])
        n = n + (b.count(per, 0) if step.r is not None else per * min(max(b.first, 0), B))
    here = 0
    for _, use, stage in MB_USES:
        if step.plus(LAG[stage]).real:
            here += 1
        if use == name:
            return n + here
    raise KeyError(name)


def ma_count(batch, name):
    return batch.count(len(MA_FILLS), MA_FILLS.index(name) + 1)


def ma_free(batch, name):
    return batch.count(len(MA_FILLS), MA_FILLS.index(name) - 1)


def steps(eng):
    for it in range(-2, 2):
        yield Batch(it)
    with eng.Fori(0, 2) as r:
        yield Batch(2, r)
        yield Batch(3, r)
    for it in range(6, B + 2):
        yield Batch(it)


def layer_kernel(nc, x, xT, wqkv, wo, wg, wu, wd, ident, cos, sin, out):
    nc.disable_value_cache = True
    with ExitStack() as ctx:
        def sb(name, shape, dt=F32):
            return ctx.enter_context(nc.sbuf_tensor(name, shape, dt))

        def ps(name, shape, dt=F32):
            return ctx.enter_context(nc.psum_tensor(name, shape, dt))

        def sem(name):
            return ctx.enter_context(nc.semaphore(name))

        wqkv_sb = sb("wqkv_sb", [P, KC, QKV])
        wo_sb = sb("wo_sb", [P, KC, D])
        wg_sb = sb("wg_sb", [P, KC, 8, P])
        wu_sb = sb("wu_sb", [P, KC, 8, P])
        wd_sb = sb("wd_sb", [P, 8, D])
        id_f = sb("id_f", [P, P])
        id_b = sb("id_b", [P, P], BF16)
        cos_sb = sb("cos_sb", [P, TT, HD])
        sin_sb = sb("sin_sb", [P, TT, HD])
        half_neg = sb("half_neg", [P, 2])
        xT_sb = sb("xT_sb", [P, KC, S])
        qk_sb = sb("qk_sb", [P, TT, QK])
        v_raw = sb("v_raw", [P, TT, KV * HD])
        rot_s = sb("rot_s", [P, TT, P])
        part = sb("part", [P, PARTS, TT, QK], BF16)
        part_T = sb("part_T", [P, len(PT_ORDER), S], BF16)
        q_stack = [sb(f"q_stack{n}", [P, H, S], BF16) for n in range(2)]
        k_stack = [sb(f"k_stack{n}", [P, KV, S], BF16) for n in range(2)]
        v_aug = [sb(f"v_aug{n}", [P, TT, KV, 32]) for n in range(2)]
        row_max = sb("row_max", [P, 2, TT, H // 2])
        max_rest = sb("max_rest", [P, TT, H // 2])
        neg_part = sb("neg_part", [P, TT, PARTS, H // 2], BF16)
        neg_T = sb("neg_T", [PARTS * H // 2, 2, S], BF16)
        prob = sb("prob", [P, 8, S])
        oT_sb = sb("oT_sb", [P, S])
        recip = sb("recip", [P, TT, 4])
        o_sb = sb("o_sb", [P, TT, D])
        feat_T = sb("feat_T", [P, KC, S])
        xr = sb("xr", [P, TT, D])
        stats = sb("stats", [P, TT, 6])
        mv = sb("mv", [P, TT, 2])
        var_eps = sb("var_eps", [P, TT])
        rstd = sb("rstd", [P, TT])
        gate = sb("gate", [P, 2, 256])
        hid = sb("hid", [P, 8, S])
        mag = sb("mag", [P, 4, 256])
        beats = sb("beats", [P, 6, 256], BF16)
        wins = sb("wins", [P, 4, 256], BF16)

        ps_m = ps("ps_m", [P, 2, 512])
        ps_s = ps("ps_s", [P, 2, 512])
        ps_o = ps("ps_o", [P, 512])
        ma = ps("ma", [P, 2, 512])
        mb = ps("mb", [P, 512])
        mb_b = mb[:, :].bitcast(BF16)

        early_in = sem("early_in")
        weights_in = sem("weights_in")
        consts_set = sem("consts_set")
        k_zeroed = sem("k_zeroed")
        xT_in = sem("xT_in")
        x_in = sem("x_in")
        ma_filled, ma_read = sem("ma_filled"), sem("ma_read")
        mb_filled, mb_read = sem("mb_filled"), sem("mb_read")
        v_built = sem("v_built")
        parts_made = sem("parts_made")
        stack_lo, stack_hi = sem("stack_lo"), sem("stack_hi")
        scored = sem("scored")
        maxed = sem("maxed")
        neg_made = sem("neg_made")
        aug_lo, aug_hi = sem("aug_lo"), sem("aug_hi")
        st_ready = sem("st_ready")
        exp_done = sem("exp_done")
        pv_done = sem("pv_done")
        oT_copied = sem("oT_copied")
        recip_made = sem("recip_made")
        summed = sem("summed")
        stat_made = sem("stat_made")
        var_made = sem("var_made")
        rstd_made = sem("rstd_made")
        ln_done = sem("ln_done")
        tanh_done = sem("tanh_done")
        gate_made = sem("gate_made")
        mag_made = sem("mag_made")
        compared = sem("compared")
        wins_made = sem("wins_made")
        sparse_made = sem("sparse_made")
        rot_step = sem("rot_step")
        neg_step = sem("neg_step")
        wins_step = sem("wins_step")
        v_zeroed = sem("v_zeroed")
        passed = sem("passed")
        out_done = sem("out_done")

        block = ctx.enter_context(nc.Block())

        @block.sync
        def _(sp):
            sp.dma_start(wqkv_sb[:], wqkv).then_inc(early_in, 16)
            sp.dma_start(xT_sb[:], xT[0]).then_inc(xT_in, 16)
            for dst, src in ((id_f, ident), (cos_sb, cos), (sin_sb, sin)):
                sp.dma_start(dst[:], src).then_inc(early_in, 16)
            for dst, src in ((wo_sb, wo), (wg_sb, wg), (wu_sb, wu), (wd_sb, wd)):
                sp.dma_start(dst[:], src).then_inc(weights_in, 16)

            def scatter(b, chunk, half, done):
                par = b.parity
                for i in range(PARTS):
                    for j in range(PARTS):
                        row = 24 * i + 8 * j
                        src = part_T[:, PT_ORDER.index((i, chunk)), :]
                        sp.dma_start(q_stack[par][row:row + 8, 16 * half:16 * half + 16, :],
                                     src).then_inc(done, 16)
                        src = part_T[32 * half:32 * half + 32, PT_ORDER.index((j, 2)), :]
                        sp.dma_start(k_stack[par][row:row + 8, 4 * half:4 * half + 4, :],
                                     src).then_inc(done, 16)

            def move_x(b, half, store):
                sl = slice(2 * half, 2 * half + 2)
                dram = (out if store else x)[b.index].rearrange("(t p) d -> p t d", p=P)[:, sl, :]
                if store:
                    sp.dma_start(dram, xr[:, sl, :]).then_inc(out_done, 16)
                else:
                    sp.dma_start(xr[:, sl, :], dram).then_inc(x_in, 16)

            for step in steps(sp):
                bA, bM, bB, bF, bE = (step.plus(LAG[s]) for s in "AMBFE")
                if bA.real and (bA.r is not None or bA.first > 0):
                    sp.wait_ge(mb_filled, mb_count(step.plus(-1), "qkv3"))
                    sp.dma_start(xT_sb[:], xT[bA.index]).then_inc(xT_in, 16)
                if bF.real:
                    sp.wait_ge(out_done, bF.count(32, -16))
                    move_x(bF, 0, False)
                if bE.real:
                    sp.wait_ge(ln_done, bE.count(8, 8))
                    move_x(bE, 1, True)
                if bF.real:
                    sp.wait_ge(out_done, bF.count(32, 0))
                    move_x(bF, 1, False)
                if bM.real:
                    sp.wait_ge(mb_read, mb_count(step.plus(-1), "pT4"))
                    sp.wait_ge(pv_done, bM.plus(-2).count(32, 32))
                    if bM.first < 2 and bM.r is None:
                        sp.wait_ge(consts_set, 3)
                    scatter(bM, 1, 1, stack_hi)
                if bB.real:
                    sp.wait_ge(mb_read, mb_count(step, "mt1"))
                    sp.dma_start(q_stack[bB.parity][AUG:AUG + 3, 16:32, :], neg_T[:, 1, :]).then_inc(aug_hi, 16)
                if bA.real:
                    sp.wait_ge(mb_read, mb_count(step, "pT2"))
                    sp.wait_ge(pv_done, bA.plus(-2).count(32, 16))
                    if bA.first < 2 and bA.r is None:
                        sp.wait_ge(consts_set, 3)
                    scatter(bA, 0, 0, stack_lo)
                if bF.real:
                    sp.wait_ge(ln_done, bF.count(8, 6))
                    move_x(bF, 0, True)
                if bM.real:
                    sp.wait_ge(mb_read, mb_count(step, "mt0"))
                    sp.dma_start(q_stack[bM.parity][AUG:AUG + 3, 0:16, :], neg_T[:, 0, :]).then_inc(aug_lo, 16)
            sp.wait_ge(out_done, 32 * B)

        @block.tensor
        def _(pe):
            pe.wait_ge(early_in, 16 * 4)

            def max_scores(b, head, qt):
                n = 4 * head + qt
                if n == 0:
                    pe.wait_ge(stack_lo, b.count(288, 288))
                if n == 64:
                    pe.wait_ge(stack_hi, b.count(288, 288))
                pe.wait_ge(maxed, b.count(128, n - 1))
                nc.tensor.matmul(ps_m[:, n % 2, :], q_stack[b.parity][0:AUG, head, qt * P:(qt + 1) * P],
                                 k_stack[b.parity][0:AUG, head // 4, :], start=True, stop=True).then_inc(scored, 1)

            def key_scores(step, slot, i):
                b = step.plus(LAG["B"])
                g, kt = slot // 4, slot % 4
                n = 4 * slot + i
                if slot == 0 and i == 0:
                    pe.wait_ge(aug_lo, b.count(16, 16))
                if slot == 16 and i == 0:
                    pe.wait_ge(aug_hi, b.count(16, 16))
                pe.wait_ge(exp_done, b.count(128, n - 1))
                nc.tensor.matmul(ps_s[:, n % 2, :], k_stack[b.parity][:, g, kt * P:(kt + 1) * P],
                                 q_stack[b.parity][:, 4 * g + i, :], start=True, stop=True).then_inc(st_ready, 1)

            def values(step, quad):
                b = step.plus(LAG["B"])
                g, kt = quad // 4, quad % 4
                if quad == 0:
                    pe.wait_ge(v_built, b.count(1, 1))
                if kt == 0:
                    pe.wait_ge(oT_copied, b.count(8, g))
                pe.wait_ge(exp_done, b.count(128, 4 * quad + 4))
                for i in range(4):
                    mm = nc.tensor.matmul(ps_o[32 * i:32 * i + 32, :], v_aug[b.parity][:, kt, g, :],
                                          prob[:, (4 * quad + i) % 8, :], start=(kt == 0), stop=(kt == 3))
                mm.then_inc(pv_done, 1)

            def side_mb(step, name, b):
                pe.wait_ge(mb_read, mb_count(step, name) - 1)
                if name.startswith("ott"):
                    g = int(name[3:])
                    pe.wait_ge(oT_copied, b.count(8, g + 1))
                    for qt in range(TT):
                        mm = nc.tensor.transpose(mb[:, qt * P:(qt + 1) * P], oT_sb[:, qt * P:(qt + 1) * P], id_f[:])
                elif name.startswith("oT"):
                    kc = int(name[2:])
                    pe.wait_ge(mb_read, mb_count(step, "ott7"))
                    for tt in range(TT):
                        mm = nc.tensor.transpose(mb[:, tt * P:(tt + 1) * P], o_sb[:, tt, kc * P:(kc + 1) * P], id_f[:])
                elif name.startswith("xT"):
                    kc = int(name[2:])
                    pe.wait_ge(ln_done, b.count(8, 4))
                    for tt in range(TT):
                        mm = nc.tensor.transpose(mb[:, tt * P:(tt + 1) * P], xr[:, tt, kc * P:(kc + 1) * P], id_f[:])
                elif name.startswith("qkv"):
                    tt = int(name[3:])
                    pe.wait_ge(xT_in, b.count(16, 16))
                    for kc in range(KC):
                        mm = nc.tensor.matmul(mb[:, 0:QKV], xT_sb[:, kc, tt * P:(tt + 1) * P], wqkv_sb[:, kc, :],
                                              start=(kc == 0), stop=(kc == KC - 1))
                elif name.startswith("pT"):
                    u = int(name[2:])
                    pe.wait_ge(consts_set, 3)
                    pe.wait_ge(parts_made, b.count(1, 1))
                    pe.sem_inc(passed, 1)
                    for k, (i, c) in enumerate(PT_ORDER[2 * u:2 * u + 2]):
                        w = P if c < 2 else KV * HD
                        for tt in range(TT):
                            mm = nc.tensor.transpose(mb_b[0:w, k * S + tt * P:k * S + (tt + 1) * P],
                                                     part[:, i, tt, c * P:c * P + w], id_b[:])
                else:
                    half = int(name[2:])
                    pe.wait_ge(neg_made, b.count(2, half + 1))
                    pe.sem_inc(passed, 1)
                    for qt in range(TT):
                        mm = nc.tensor.transpose(mb_b[0:PARTS * H // 2, qt * P:(qt + 1) * P],
                                                 neg_part[:, qt, :, :].rearrange("p a h -> p (a h)"), id_b[:])
                mm.then_inc(mb_filled, 1)

            def project(step, b, slot, i):
                use, tt, kc = slot - WO_SLOT, 2 * (slot - WO_SLOT) + i // 2, i % 2
                name = f"wo{use}"
                if i == 0:
                    pe.wait_ge(weights_in, 16 * 4)
                    pe.wait_ge(ma_read, ma_free(b, name))
                    pe.wait_ge(mb_read, mb_count(step, "oT1"))
                mm = nc.tensor.matmul(ma[:, use % 2, (tt % 2) * D:(tt % 2 + 1) * D], feat_T[:, kc, tt * P:(tt + 1) * P],
                                      wo_sb[:, kc, :], start=(kc == 0), stop=(kc == KC - 1))
                if i == 3:
                    mm.then_inc(ma_filled, 1)

            def gate_up(step, b, slot, i):
                f = slot - GU_SLOT
                u, j, kc = f // 4, f % 4, i % 2
                half, t = u // 2, u % 2
                if i == 0:
                    pe.wait_ge(ma_read, ma_free(b, f"gu{f}"))
                if f == 0 and i == 0:
                    pe.wait_ge(mb_read, mb_count(step, "xT1"))
                mm = nc.tensor.matmul(ma[:, f % 2, (i // 2) * 256:(i // 2 + 1) * 256],
                                      (wg_sb, wu_sb)[i // 2][:, kc, 4 * t + j, :],
                                      feat_T[:, kc, half * 256:(half + 1) * 256], start=(kc == 0), stop=(kc == KC - 1))
                if i == 3:
                    mm.then_inc(ma_filled, 1)

            def down(b, slot, i):
                tt, n = (slot - DN_SLOT) // 2, 4 * ((slot - DN_SLOT) % 2) + i
                if n == 0 and tt % 2 == 0:
                    pe.wait_ge(ma_read, ma_free(b, f"dn{tt // 2}"))
                    pe.wait_ge(sparse_made, b.count(4, tt + 2))
                mm = nc.tensor.matmul(ma[:, tt // 2, (tt % 2) * D:(tt % 2 + 1) * D], hid[:, n, tt * P:(tt + 1) * P],
                                      wd_sb[:, n, :], start=(n == 0), stop=(n == 7))
                if n == 7 and tt % 2 == 1:
                    mm.then_inc(ma_filled, 1)

            for step in steps(pe):
                bM, bB, bF = (step.plus(LAG[s]) for s in "MBF")
                for slot in range(SLOTS):
                    for i in range(4):
                        if bB.real:
                            key_scores(step, slot, i)
                        if slot < H - LEAD and bB.real:
                            max_scores(bB, slot + LEAD, i)
                        if slot >= H - LEAD and bM.real:
                            max_scores(bM, slot + LEAD - H, i)
                        if bF.real and WO_SLOT <= slot < WO_SLOT + 2:
                            project(step, bF, slot, i)
                        if bF.real and GU_SLOT <= slot < GU_SLOT + 16:
                            gate_up(step, bF, slot, i)
                        if bF.real and DN_SLOT <= slot < DN_SLOT + 8:
                            down(bF, slot, i)
                        for at, name, stage in MB_USES:
                            b = step.plus(LAG[stage])
                            if at == (slot, i) and b.real:
                                side_mb(step, name, b)
                    if bB.real and slot >= 1:
                        values(step, slot - 1)
                if bB.real:
                    values(step, SLOTS - 1)

        @block.scalar
        def _(act):
            act.wait_ge(early_in, 16 * 4)
            nc.scalar.mul(q_stack[1][:].bitcast(F32).rearrange("p h t -> p (h t)"),
                          id_f[:, 0:1].broadcast_to([P, H * S // 2]), 0.0).then_inc(consts_set, 1)

            def exps(step, slot, i):
                b = step.plus(LAG["B"])
                n = 4 * slot + i
                if i == 0:
                    act.wait_ge(pv_done, b.count(32, slot - 1))
                act.wait_ge(st_ready, b.count(128, n + 1))
                nc.scalar.activation(prob[:, n % 8, :], ps_s[:, n % 2, :], ACT.Exp, scale=SCALE).then_inc(exp_done, 1)

            def output_copy(b, g, last_use):
                act.wait_ge(pv_done, b.count(32, 4 * g + 4))
                if last_use is not None:
                    act.wait_ge(mb_filled, last_use)
                nc.scalar.copy(oT_sb[:], ps_o[:]).then_inc(oT_copied, 1)

            def side(step, slot, i):
                for at, name, stage in MB_USES:
                    b = step.plus(LAG[stage])
                    if at != (slot, i) or not b.real or name.startswith("ott"):
                        continue
                    act.wait_ge(mb_filled, mb_count(step, name))
                    if name.startswith("qkv"):
                        tt = int(name[3:])
                        if tt == 0:
                            act.wait_ge(parts_made, b.count(1, 0))
                            act.wait_ge(v_built, b.count(1, 0))
                        nc.scalar.copy(v_raw[:, tt, :], mb[:, QK:QKV])
                        nc.scalar.copy(qk_sb[:, tt, :], mb[:, 0:QK]).then_inc(mb_read, 1)
                    elif name.startswith("pT"):
                        u = int(name[2:])
                        if u == 0:
                            act.wait_ge(stack_lo, b.count(288, 0))
                            act.wait_ge(stack_hi, b.count(288, 0))
                        chunks = PT_ORDER[2 * u:2 * u + 2]
                        if len({c < 2 for _, c in chunks}) == 1:
                            w = P if chunks[0][1] < 2 else KV * HD
                            cp = nc.scalar.copy(part_T[0:w, 2 * u:2 * u + len(chunks), :],
                                                mb_b[0:w, 0:len(chunks) * S].rearrange("p (k t) -> p k t", t=S))
                            cp.then_inc(mb_read, 1)
                        else:
                            nc.scalar.copy(part_T[0:P, 2 * u, :], mb_b[0:P, 0:S])
                            nc.scalar.copy(part_T[0:KV * HD, 2 * u + 1, :], mb_b[0:KV * HD, S:2 * S]).then_inc(mb_read, 1)
                    elif name.startswith("mt"):
                        half_of = int(name[2:])
                        act.wait_ge(aug_hi if half_of else aug_lo, b.count(16, 0))
                        n = PARTS * H // 2
                        nc.scalar.copy(neg_T[:, half_of, :], mb_b[0:n, 0:S]).then_inc(mb_read, 1)
                    else:
                        kc = int(name[2:])
                        if name.startswith("xT"):
                            act.wait_ge(ma_filled, ma_count(b, "wo1"))
                        nc.scalar.copy(feat_T[:, kc, :], mb[:, :]).then_inc(mb_read, 1)

            for step in steps(act):
                bB, bF = step.plus(LAG["B"]), step.plus(LAG["F"])
                for slot in range(SLOTS):
                    if slot == 1 and bF.real:
                        output_copy(bF, 7, mb_count(step.plus(-1), "ott6"))
                    if slot % 4 == 1 and slot >= 5 and bB.real:
                        g = slot // 4 - 1
                        prev = f"ott{g - 1}" if g else "ott7"
                        output_copy(bB, g, mb_count(step, prev) if g or bF.real else None)
                    for i in range(4):
                        if bB.real:
                            exps(step, slot, i)
                        if i == 0 and GU_SLOT < slot <= GU_SLOT + 16 and bF.real:
                            f = slot - GU_SLOT - 1
                            act.wait_ge(ma_filled, ma_count(bF, f"gu{f}"))
                            nc.scalar.activation(gate[:, f % 2, :], ma[:, f % 2, 0:256], ACT.Tanh,
                                                 scale=0.5).then_inc(tanh_done, 1)
                        if i == 2 and slot in (12, 16, 20, 24) and bF.real:
                            u = (slot - 12) // 4
                            act.wait_ge(ma_read, ma_count(bF, f"gu{4 * u + 3}"))
                            act.wait_ge(compared, bF.count(4, u))
                            nc.scalar.activation(mag[:], hid[:, 4 * (u % 2):4 * (u % 2) + 4,
                                                             256 * (u // 2):256 * (u // 2) + 256],
                                                 ACT.Abs).then_inc(mag_made, 1)
                        side(step, slot, i)

        @block.vector
        def _(dve):
            for n in range(2):
                nc.vector.memset(k_stack[n][:].bitcast(F32), 0.0).then_inc(k_zeroed, 1)
            dve.wait_ge(k_zeroed, 2)
            for n in range(2):
                nc.vector.memset(k_stack[n][AUG:AUG + 3, :, :], 1.0)
            nc.vector.memset(q_stack[0][:].bitcast(F32), 0.0)
            dve.wait_ge(early_in, 16 * 4)
            nc.vector.tensor_copy(id_b[:], id_f[:]).then_inc(consts_set, 1)

            def row_maximum(b, head, qt):
                n = 4 * head + qt
                if n == 0:
                    dve.wait_ge(neg_made, b.count(2, -1))
                if n == 64:
                    dve.wait_ge(neg_made, b.count(2, 0))
                dve.wait_ge(scored, b.count(128, n + 1))
                nc.vector.tensor_reduce(row_max[:, head // 16, qt, head % 16:head % 16 + 1], ps_m[:, n % 2, :],
                                        AX.X, ALU.max).then_inc(maxed, 1)

            def normalise_group(step, b, name):
                g = int(name[3:])
                dve.wait_ge(mb_filled, mb_count(step, name))
                t = mb[:, :].rearrange("p (t i c) -> p t i c", t=TT, i=4)
                nc.vector.reciprocal(recip[:], t[:, :, :, HD]).then_inc(recip_made, 1)
                dve.wait_ge(recip_made, b.count(8, g + 1))
                nc.vector.tensor_tensor(o_sb[:, :, 32 * g:32 * g + 32].rearrange("p t (i d) -> p t i d", i=4),
                                        t[:, :, :, 0:HD], recip[:].unsqueeze(3).broadcast_to([P, TT, 4, HD]),
                                        ALU.mult).then_inc(mb_read, 1)

            def residual(b, which, half, name):
                dve.wait_ge(ma_filled, ma_count(b, name))
                sl = xr[:, 2 * half:2 * half + 2, :]
                nc.vector.tensor_tensor(sl, ma[:, half, :].rearrange("p (k d) -> p k d", k=2), sl, ALU.add).then_inc(ma_read, 1)
                dve.wait_ge(ma_read, ma_count(b, name))
                for k in range(2):
                    tt = 2 * half + k
                    nc.vector.bn_stats(stats[:, tt, :], xr[:, tt, :]).then_inc(summed, 1)
                    dve.wait_ge(summed, b.count(8, 4 * which + tt + 1))
                    dve.sem_inc(passed, 1)
                    nc.vector.bn_aggr(mv[:, tt, :], stats[:, tt, :]).then_inc(stat_made, 1)

            def normalise(b, which, tiles):
                for tt in tiles:
                    dve.wait_ge(rstd_made, b.count(4, 2 * which + tt // 2 + 1))
                    nc.vector.tensor_scalar(xr[:, tt, :], xr[:, tt, :], mv[:, tt, 0:1], rstd[:, tt:tt + 1],
                                            ALU.subtract, ALU.mult).then_inc(ln_done, 1)

            def swiglu(b, f):
                u, j = f // 4, f % 4
                half, t = u // 2, u % 2
                dve.wait_ge(tanh_done, b.count(16, f + 1))
                g = gate[:, f % 2, :]
                nc.vector.scalar_tensor_tensor(out=g, in0=g, scalar=1.0, in1=ma[:, f % 2, 0:256],
                                               op0=ALU.add, op1=ALU.mult).then_inc(gate_made, 1)
                dve.wait_ge(gate_made, b.count(16, f + 1))
                nc.vector.scalar_tensor_tensor(out=hid[:, 4 * t + j, half * 256:(half + 1) * 256], in0=g,
                                               scalar=0.5, in1=ma[:, f % 2, 256:512], op0=ALU.mult,
                                               op1=ALU.mult).then_inc(ma_read, 1)

            def compare(b, u):
                dve.wait_ge(mag_made, b.count(4, u + 1))
                dve.wait_ge(wins_made, b.count(4, u))
                nc.vector.tensor_tensor(beats[:, 0:2, :], mag[:, 0:4:2, :], mag[:, 1:4:2, :], ALU.is_ge)
                nc.vector.tensor_tensor(beats[:, 2:4, :], mag[:, 0:2, :], mag[:, 2:4, :], ALU.is_ge)
                nc.vector.tensor_tensor(beats[:, 4, :], mag[:, 0, :], mag[:, 3, :], ALU.is_ge)
                nc.vector.tensor_tensor(beats[:, 5, :], mag[:, 1, :], mag[:, 2, :], ALU.is_ge).then_inc(compared, 1)

            def sparsify(b, u):
                dve.wait_ge(wins_made, b.count(4, u + 1))
                half, t = u // 2, u % 2
                for j, (op, bound) in enumerate(((ALU.is_ge, 2.0), (ALU.is_ge, 1.0), (ALU.is_ge, 0.0), (ALU.is_le, 1.0))):
                    h = hid[:, 4 * t + j, half * 256:(half + 1) * 256]
                    last = nc.vector.scalar_tensor_tensor(out=h, in0=wins[:, j, :], scalar=bound, in1=h,
                                                          op0=op, op1=ALU.mult)
                last.then_inc(sparse_made, 1)

            for step in steps(dve):
                bM, bB, bF, bE = (step.plus(LAG[s]) for s in "MBFE")
                for slot in range(SLOTS):
                    if slot == 0 and bE.real:
                        normalise(bE, 1, (2, 3))
                    for i in range(4):
                        if slot < H - LEAD and bB.real:
                            row_maximum(bB, slot + LEAD, i)
                        if slot >= H - LEAD and bM.real:
                            row_maximum(bM, slot + LEAD - H, i)
                        for at, name, stage in MB_USES:
                            b = step.plus(LAG[stage])
                            if at == (slot, i) and b.real and name.startswith("ott"):
                                if name == "ott0" and bF.real:
                                    dve.wait_ge(mb_filled, mb_count(step, "oT1"))
                                normalise_group(step, b, name)
                        if not bF.real:
                            continue
                        if i == 1 and slot == WO_SLOT + 1:
                            dve.wait_ge(x_in, bF.count(32, 32))
                            residual(bF, 0, 0, "wo0")
                        if i == 1 and slot == WO_SLOT + 2:
                            residual(bF, 0, 1, "wo1")
                        if i == 3 and slot == WO_SLOT + 2:
                            normalise(bF, 0, range(TT))
                        if i == 1 and GU_SLOT < slot <= GU_SLOT + 16:
                            swiglu(bF, slot - GU_SLOT - 1)
                        if i == 3 and slot in (12, 16, 20, 24):
                            compare(bF, (slot - 12) // 4)
                        if i == 3 and slot in (14, 18, 22, 26):
                            sparsify(bF, (slot - 14) // 4)
                        if i == 1 and slot == DN_SLOT + 4:
                            residual(bF, 1, 0, "dn0")
                        if i == 1 and slot == DN_SLOT + 5:
                            normalise(bF, 1, (0, 1))
                        if i == 1 and slot == DN_SLOT + 8:
                            residual(bF, 1, 1, "dn1")

        @block.gpsimd
        def _(pool):
            for n in range(2):
                nc.gpsimd.memset(v_aug[n][:], 0.0).then_inc(v_zeroed, 1)
            nc.gpsimd.memset(half_neg[:], -0.5)
            pool.wait_ge(v_zeroed, 2)
            nc.gpsimd.memset(v_aug[0][:, :, :, HD:HD + 1], 1.0)
            nc.gpsimd.memset(v_aug[1][:, :, :, HD:HD + 1], 1.0).then_inc(consts_set, 1)
            pool.wait_ge(early_in, 16 * 4)

            def build_v(step, b):
                pool.wait_ge(mb_read, mb_count(step.plus(-1), "qkv3"))
                pool.wait_ge(pv_done, b.plus(-2).count(32, 32))
                pool.sem_inc(passed, 1)
                nc.gpsimd.tensor_copy(v_aug[b.parity][:, :, :, 0:HD],
                                      v_raw[:].rearrange("p t (k d) -> p t k d", d=HD)).then_inc(v_built, 1)

            def split_negated(b, half, last_transposed):
                m = row_max[:, half]
                if last_transposed is not None:
                    pool.wait_ge(mb_filled, last_transposed)
                pool.wait_ge(maxed, b.count(128, 64 * (half + 1)))
                pool.sem_inc(passed, 1)
                k = 4 * half
                nc.gpsimd.tensor_scalar(neg_part[:, :, 0, :], m, -1.0, None, ALU.mult).then_inc(neg_step, 1)
                pool.wait_ge(neg_step, b.count(8, k + 1))
                nc.gpsimd.tensor_tensor(max_rest[:], m, neg_part[:, :, 0, :], ALU.add).then_inc(neg_step, 1)
                pool.wait_ge(neg_step, b.count(8, k + 2))
                pool.sem_inc(passed, 1)
                nc.gpsimd.tensor_scalar(neg_part[:, :, 1, :], max_rest[:], -1.0, None, ALU.mult).then_inc(neg_step, 1)
                pool.wait_ge(neg_step, b.count(8, k + 3))
                nc.gpsimd.tensor_tensor(max_rest[:], max_rest[:], neg_part[:, :, 1, :], ALU.add).then_inc(neg_step, 1)
                pool.wait_ge(neg_step, b.count(8, k + 4))
                pool.sem_inc(passed, 1)
                nc.gpsimd.tensor_scalar(neg_part[:, :, 2, :], max_rest[:], -1.0, None, ALU.mult).then_inc(neg_made, 1)

            def inverse_std(b, which, half):
                k = 2 * which + half + 1
                pool.wait_ge(stat_made, b.count(8, 2 * k))
                pool.sem_inc(passed, 1)
                sl = slice(2 * half, 2 * half + 2)
                nc.gpsimd.tensor_scalar(var_eps[:, sl], mv[:, sl, 1], EPS, None, ALU.add).then_inc(var_made, 1)
                pool.wait_ge(var_made, b.count(4, k))
                nc.gpsimd.tensor_tensor(rstd[:, sl], var_eps[:, sl], half_neg[:], ALU.pow).then_inc(rstd_made, 1)

            def rotate_and_split(step, b):
                pool.wait_ge(mb_read, mb_count(step, "qkv3"))
                if not (b.r is None and b.first == 0):
                    pool.wait_ge(mb_filled, mb_count(step.plus(-1), "pT4"))
                n = 0
                for off, w in ((0, P), (P, P), (2 * P, 32), (2 * P + 32, 32)):
                    q = qk_sb[:, :, off:off + w].rearrange("p t (d h) -> p t d h", d=HD)
                    heads = w // HD
                    s = rot_s[:, :, 0:w].rearrange("p t (d h) -> p t d h", d=HD)
                    c_ = cos_sb[:].unsqueeze(3).broadcast_to([P, TT, HD, heads])
                    s_ = sin_sb[:].unsqueeze(3).broadcast_to([P, TT, HD, heads])
                    nc.gpsimd.tensor_tensor(s[:, :, 0:4], q[:, :, 4:8], s_[:, :, 0:4], ALU.mult)
                    nc.gpsimd.tensor_tensor(s[:, :, 4:8], q[:, :, 0:4], s_[:, :, 4:8], ALU.mult).then_inc(rot_step, 1)
                    n += 1
                    pool.wait_ge(rot_step, b.count(16, n))
                    nc.gpsimd.tensor_tensor(q, q, c_, ALU.mult).then_inc(rot_step, 1)
                    n += 1
                    pool.wait_ge(rot_step, b.count(16, n))
                    nc.gpsimd.tensor_tensor(q, q, s, ALU.add).then_inc(rot_step, 1)
                    n += 1
                    if n < 12:
                        pool.wait_ge(rot_step, b.count(16, n))
                pool.wait_ge(rot_step, b.count(16, n))
                pool.sem_inc(passed, 1)
                for i in range(PARTS):
                    cast = nc.gpsimd.tensor_copy(part[:, i], qk_sb[:])
                    if i == PARTS - 1:
                        cast.then_inc(parts_made, 1)
                        break
                    cast.then_inc(rot_step, 1)
                    n += 1
                    pool.wait_ge(rot_step, b.count(16, n))
                    nc.gpsimd.tensor_tensor(qk_sb[:], qk_sb[:], part[:, i], ALU.subtract).then_inc(rot_step, 1)
                    n += 1
                    pool.wait_ge(rot_step, b.count(16, n))
                    pool.sem_inc(passed, 1)
                assert n == 16

            def count_wins(b, u):
                pool.wait_ge(compared, b.count(4, u + 1))
                pool.wait_ge(sparse_made, b.count(4, u))
                m01, m23, m02, m13, m03, m12 = (beats[:, k, :] for k in range(6))
                nc.gpsimd.tensor_tensor(wins[:, 0, :], m02, m03, ALU.add)
                nc.gpsimd.tensor_tensor(wins[:, 1, :], m13, m12, ALU.add)
                nc.gpsimd.tensor_tensor(wins[:, 2, :], m02, m12, ALU.add)
                nc.gpsimd.tensor_tensor(wins[:, 3, :], m03, m13, ALU.add).then_inc(wins_step, 1)
                pool.wait_ge(wins_step, b.count(4, u + 1))
                nc.gpsimd.tensor_tensor(wins[:, 0, :], wins[:, 0, :], m01, ALU.add)
                nc.gpsimd.tensor_tensor(wins[:, 1, :], wins[:, 1, :], m01, ALU.subtract)
                nc.gpsimd.tensor_tensor(wins[:, 2, :], m23, wins[:, 2, :], ALU.subtract)
                nc.gpsimd.tensor_tensor(wins[:, 3, :], wins[:, 3, :], m23, ALU.add).then_inc(wins_made, 1)

            for step in steps(pool):
                bA, bM, bB, bF = (step.plus(LAG[s]) for s in "AMBF")
                if bM.real:
                    build_v(step, bM)
                if bF.real:
                    inverse_std(bF, 0, 0)
                    inverse_std(bF, 0, 1)
                if bA.real:
                    rotate_and_split(step, bA)
                if bB.real:
                    split_negated(bB, 1, mb_count(step.plus(-1), "mt0"))
                if bF.real:
                    for u in range(4):
                        count_wins(bF, u)
                    inverse_std(bF, 1, 0)
                if bM.real:
                    split_negated(bM, 0, mb_count(step, "mt1") if bB.real else None)
                if bF.real:
                    inverse_std(bF, 1, 1)


def kernel(L0_attn_x, L0_attn_Wq, L0_attn_Wk, L0_attn_Wv, L0_attn_Wo, L0_ffn_w_gate, L0_ffn_w_up, L0_ffn_w_down):
    import concourse.bacc as _bacc
    from concourse.bass_utils import run_bass_kernel_spmd as _run

    x = np.asarray(L0_attn_x)
    wq = np.asarray(L0_attn_Wq).reshape(2, H // 2, HD, D).transpose(0, 2, 1, 3).reshape(H * HD, D)
    wk = np.asarray(L0_attn_Wk).reshape(2, KV // 2, HD, D).transpose(0, 2, 1, 3).reshape(KV * HD, D)
    wqkv = np.concatenate([wq, wk, np.asarray(L0_attn_Wv)], axis=0)

    def chunks(w):
        return w.reshape(KC, P, -1).transpose(1, 0, 2)

    def hidden_tiles(w):
        return w.reshape(KC, P, 2, P, 4).transpose(1, 0, 2, 4, 3).reshape(P, KC, 8, P)

    inv = (1.0 / np.float32(10000.0) ** (np.arange(0, HD, 2, dtype=np.float32) / HD)).astype(np.float32)
    ang = np.arange(S, dtype=np.float32)[:, None] * inv[None, :]
    cos = np.concatenate([np.cos(ang), np.cos(ang)], axis=1).reshape(TT, P, HD).transpose(1, 0, 2)
    sin = np.concatenate([-np.sin(ang), np.sin(ang)], axis=1).reshape(TT, P, HD).transpose(1, 0, 2)
    data = {
        "x": x,
        "xT": x.reshape(B, S, KC, P).transpose(0, 3, 2, 1),
        "wqkv": chunks(wqkv.T),
        "wo": chunks(np.asarray(L0_attn_Wo).T),
        "wg": hidden_tiles(np.asarray(L0_ffn_w_gate)),
        "wu": hidden_tiles(np.asarray(L0_ffn_w_up)),
        "wd": np.asarray(L0_ffn_w_down).reshape(2, P, 4, D).transpose(1, 0, 2, 3).reshape(P, 8, D),
        "ident": np.eye(P, dtype=np.float32),
        "cos": cos, "sin": sin,
    }
    nc = _bacc.Bacc("TRN2", target_bir_lowering=False, num_devices=1)
    arrays, args = {}, []
    for name, a in data.items():
        a = np.ascontiguousarray(a)
        arrays[f"in_{name}"] = a
        args.append(nc.dram_tensor(f"in_{name}", a.shape, mybir.dt.from_np(a.dtype), kind="ExternalInput").ap())
    args.append(nc.dram_tensor("out_0", (B, S, D), F32, kind="ExternalOutput").ap())
    layer_kernel(nc, *args)
    return _run(nc, [arrays], core_ids=[0]).results[0]["out_0"]
```

```python
from contextlib import ExitStack

import numpy as np

import concourse.bass as bass
from concourse import mybir

F32 = mybir.dt.float32
BF16 = mybir.dt.bfloat16
F32R = mybir.dt.float32r
ALU = mybir.AluOpType
ACT = mybir.ActivationFunctionType
AX = mybir.AxisListType

P = 128
B, S, D = 8, 512, 256
H, KV, HD = 32, 8, 8
TT = S // P
KC = D // P
QK = (H + KV) * HD
QKV = QK + KV * HD
SLOTS = 32
PARTS = 3
AUG = 96
SCALE = HD ** -0.5
EPS = 1e-5
LEAD = 12

HALF = S // 2
WINDOW = (19, 3)
WO_AT, NORM_AT, REST_AT, GU_AT, DN_AT, DN_END = 0, 2, 5, 6, 17, 22
MAG_AT, WINS_AT = (10, 14), (12, 15)
COMPARE_AT = (((10, 3), (11, 3), (12, 0)), ((15, 0), (15, 1), (15, 3)))
SPARSE_AT = (((13, 1), (13, 3), (14, 1), (14, 3)), ((17, 0), (17, 1), (17, 2), (17, 3)))

MB_USES = [
    ((0, 0), "qkv0", "A"), ((0, 3), "qkv1", "A"), ((1, 1), "qkv2", "A"), ((1, 2), "ott7", "F"),
    ((2, 1), "qkv3", "A"), ((2, 2), "oT1", "F"), ((5, 3), "mt1", "B"), ((6, 0), "ott0", "B"),
    ((7, 3), "xT1", "F"), ((10, 0), "ott1", "B"), ((12, 1), "pT0", "A"), ((12, 3), "pT1", "A"),
    ((13, 3), "mt2", "B"), ((14, 0), "ott2", "B"), ((14, 2), "pT2", "A"), ((15, 2), "pT3", "A"),
    ((16, 2), "pT4", "A"), ((17, 2), "ott3", "B"), ((18, 2), "oT0", "B"), ((21, 3), "mt3", "B"),
    ((22, 0), "ott4", "B"), ((23, 2), "xT0", "B"), ((26, 0), "ott5", "B"), ((29, 1), "mt0", "M"),
    ((30, 0), "ott6", "B"),
]
PT_ORDER = [(0, 0), (1, 0), (2, 0), (0, 2), (1, 2), (2, 2), (0, 1), (1, 1), (2, 1)]
LAG = {"A": 1, "M": 1, "B": 0, "F": -1}


ROPE_CHUNKS = ((0, P), (P, P), (2 * P, 32), (2 * P + 32, 32))


def max_tile(n):
    q, r = n // 32, n % 32
    return 16 * (q % 2) + r // 2, 2 * (q // 2) + r % 2


def key_tile(slot, i):
    eight = slot // 4 % 4
    return 2 * eight + i // 2, i % 2, slot % 4, slot // 16


class Batch:

    def __init__(self, first, r=None, stride=2):
        self.first, self.r, self.stride = first, r, stride

    def plus(self, n):
        return Batch(self.first + n, self.r, self.stride)

    @property
    def real(self):
        return self.r is not None or 0 <= self.first < B

    @property
    def parity(self):
        return self.first % 2

    def count(self, per, more):
        v = self.first * per + more
        return max(v, 0) if self.r is None else v + self.r * (self.stride * per)

    @property
    def index(self):
        return self.count(1, 0)


def mb_count(step, name):
    n = 0
    for stage in "AMBF":
        per = sum(1 for _, _, s in MB_USES if s == stage)
        b = step.plus(LAG[stage])
        n = n + (b.count(per, 0) if step.r is not None else per * min(max(b.first, 0), B))
    here = 0
    for _, use, stage in MB_USES:
        if step.plus(LAG[stage]).real:
            here += 1
        if use == name:
            return n + here
    raise KeyError(name)


class Unit:

    def __init__(self, batch, half):
        self.batch, self.half = batch, half

    @property
    def real(self):
        return self.batch.real

    @property
    def last(self):
        return self.batch.r is None and (self.batch.first, self.half) == (B - 1, 1)

    @property
    def alone(self):
        return self.batch.r is None and self.batch.first == B - 1

    def count(self, per, more):
        return self.batch.count(2 * per, per * self.half + more)


def units(step, slot):
    last, this = step.plus(-1), step
    for unit, at in ((Unit(last, 0), slot + SLOTS - WINDOW[0]), (Unit(last, 1), slot - WINDOW[1]),
                     (Unit(this, 0), slot - WINDOW[0])):
        if unit.real:
            yield unit, at


def ma_bank(unit, name):
    if name == "dn":
        return 1 if unit.last else 0
    return 1 if name == "wo" else (int(name[2:]) + 1) % 2


def ma_count(unit, name):
    at = {"wo": 0, "dn": 11}[name] if name in ("wo", "dn") else 2 + int(name[2:])
    v = unit.count(10, at)
    return v if unit.batch.r is not None else min(max(v, 1), 20 * B)


def ma_free(unit, name):
    v = ma_count(unit, name) - 2
    return v if unit.batch.r is not None else max(v, 0)


def steps(eng):
    for it in range(-1, 2):
        yield Batch(it)
    with eng.Fori(0, 2) as r:
        yield Batch(2, r)
        yield Batch(3, r)
    for it in range(6, B + 1):
        yield Batch(it)


def layer_kernel(nc, x, xT, wqkv, wo, wg, wu, wd, ident, cos, sin, out):
    nc.disable_value_cache = True
    with ExitStack() as ctx:
        def sb(name, shape, dt=F32):
            return ctx.enter_context(nc.sbuf_tensor(name, shape, dt))

        def ps(name, shape, dt=F32):
            return ctx.enter_context(nc.psum_tensor(name, shape, dt))

        def sem(name):
            return ctx.enter_context(nc.semaphore(name))

        wqkv_sb = sb("wqkv_sb", [P, KC, QKV])
        wo_sb = sb("wo_sb", [P, KC, D])
        wgu_sb = sb("wgu_sb", [P, 2, 2, KC, 8, P], F32R)
        wd_sb = sb("wd_sb", [P, 8, D])
        id_f = sb("id_f", [P, P])
        id_b = sb("id_b", [P, P], BF16)
        cos_sb = sb("cos_sb", [P, TT, HD])
        sin_sb = sb("sin_sb", [P, TT, HD])
        half_neg = sb("half_neg", [P, 2])
        v_raw = sb("v_raw", [P, TT, KV * HD])
        rot_s = [sb(f"rot_s{n}", [P, TT, w]) for n, w in enumerate((P, 32))]
        part = sb("part", [P, PARTS, TT, QK], BF16)
        part_T = sb("part_T", [P, len(PT_ORDER), S], BF16)
        xT_sb = part[:].rearrange("p i t f -> p (i t f)")[:, 0:2 * KC * S].bitcast(F32).rearrange("p (k s) -> p k s", k=KC)
        q_stack = [sb(f"q_stack{n}", [P, H, S], BF16) for n in range(2)]
        k_stack = [sb(f"k_stack{n}", [P, KV, S], BF16) for n in range(2)]
        v_aug = [sb(f"v_aug{n}", [P, TT, KV, 32]) for n in range(2)]
        row_max = sb("row_max", [P, 2, 2, H // 2])
        max_rest = sb("max_rest", [P, 2, H // 2])
        neg_part = sb("neg_part", [P, 2, PARTS, H // 2], BF16)
        neg_T = sb("neg_T", [PARTS * H // 2, 2, HALF], BF16)
        prob = sb("prob", [P, 8, S])
        oT_sb = sb("oT_sb", [P, S])
        recip = sb("recip", [P, 2, 8])
        o_sb = sb("o_sb", [P, 2, D])
        feat_high = sb("feat_high", [P, KC, HALF], F32R)
        feat_rest = sb("feat_rest", [P, KC, HALF], F32R)
        xr = sb("xr", [P, TT, D])
        stats = sb("stats", [P, TT, 6])
        mv = sb("mv", [P, TT, 2])
        var_eps = sb("var_eps", [P, TT])
        rstd = sb("rstd", [P, TT])
        gate = sb("gate", [P, 2, HALF])
        attn_T = gate
        hid = sb("hid", [P, 8, HALF])
        mag = sb("mag", [P, 4, HALF])
        beats = sb("beats", [P, 6, HALF], BF16)
        wins = sb("wins", [P, 4, HALF], BF16)

        def gu_in(r):
            return prob[:, 4 * r:4 * r + 4, :].rearrange("p n t -> p (n t)").rearrange("p (k f m) -> p k f m", k=KC, f=8)

        ps_m = ps("ps_m", [P, 2, 512])
        ps_s = ps("ps_s", [P, 2, 512])
        ps_o = ps("ps_o", [P, 512])
        ma = ps("ma", [P, 2, 512])
        mb = ps("mb", [P, 512])
        mb_b = mb[:, :].bitcast(BF16)

        def qk_of(b):
            if b.r is None and b.first == 0:
                return hid[:].rearrange("p n t -> p (n t)")[:, 0:TT * QK].rearrange("p (t f) -> p t f", t=TT)
            flat = part_T[:].rearrange("p c s -> p (c s)")[:, 0:2 * TT * QK].bitcast(F32)
            return flat.rearrange("p (t f) -> p t f", t=TT)

        def qkv_bank(b, tt):
            return (mb, ps_o, ps_s[:, 0, :], ps_s[:, 1, :])[tt] if b.r is None and b.first == 0 else mb

        early_in = sem("early_in")
        weights_in = sem("weights_in")
        consts_set = sem("consts_set")
        stack_set = [sem("stack_set0"), sem("stack_set1")]
        zeroed = sem("zeroed")
        weights_split = sem("weights_split")
        weights_high = sem("weights_high")
        high_made = sem("high_made")
        xT_in = sem("xT_in")
        x_in = sem("x_in")
        ma_filled, ma_read = sem("ma_filled"), sem("ma_read")
        mb_filled, mb_read = sem("mb_filled"), sem("mb_read")
        v_built = sem("v_built")
        parts_made = sem("parts_made")
        first_q = sem("first_q")
        first_q_step = sem("first_q_step")
        first_k_step = sem("first_k_step")
        stack_in = [sem("stack_in0"), sem("stack_in1")]
        scored = sem("scored")
        maxed = sem("maxed")
        neg_made = sem("neg_made")
        aug_in = [sem("aug_in0"), sem("aug_in1")]
        st_ready = sem("st_ready")
        exp_done = sem("exp_done")
        pv_done = sem("pv_done")
        oT_copied = sem("oT_copied")
        recip_made = sem("recip_made")
        summed = [sem("summed1"), sem("summed2")]
        stat_made = [sem("stat_made1"), sem("stat_made2")]
        var_made = [sem("var_made1"), sem("var_made2")]
        rstd_made = [sem("rstd_made1"), sem("rstd_made2")]
        ln_done = [sem("ln_done1"), sem("ln_done2")]
        tanh_done = sem("tanh_done")
        gate_made = sem("gate_made")
        mag_made = sem("mag_made")
        compared = sem("compared")
        wins_made = sem("wins_made")
        sparse_made = sem("sparse_made")
        rot_step = sem("rot_step")
        neg_step = sem("neg_step")
        wins_step = sem("wins_step")
        v_zeroed = sem("v_zeroed")
        passed = sem("passed")
        out_done = sem("out_done")

        block = ctx.enter_context(nc.Block())

        def rotate(eng, ops, qk, chunk, done, n):
            off, w = ROPE_CHUNKS[chunk]
            q = qk[:, :, off:off + w].rearrange("p t (d h) -> p t d h", d=HD)
            heads = w // HD
            s = rot_s[chunk // 2][:, :, 0:w].rearrange("p t (d h) -> p t d h", d=HD)
            c_ = cos_sb[:].unsqueeze(3).broadcast_to([P, TT, HD, heads])
            s_ = sin_sb[:].unsqueeze(3).broadcast_to([P, TT, HD, heads])
            eng.wait_ge(done, n)
            ops.tensor_tensor(s[:, :, 0:4], q[:, :, 4:8], s_[:, :, 0:4], ALU.mult)
            ops.tensor_tensor(s[:, :, 4:8], q[:, :, 0:4], s_[:, :, 4:8], ALU.mult).then_inc(done, 1)
            eng.wait_ge(done, n + 1)
            ops.tensor_tensor(q, q, c_, ALU.mult).then_inc(done, 1)
            eng.wait_ge(done, n + 2)
            ops.tensor_tensor(q, q, s, ALU.add).then_inc(done, 1)

        def split(eng, ops, qk, cols, done, n, made):
            q = qk[:, :, cols]
            for i in range(PARTS):
                eng.wait_ge(done, n + 2 * i)
                eng.sem_inc(passed, 1)
                cast = ops.tensor_copy(part[:, i, :, cols], q)
                if i == PARTS - 1:
                    cast.then_inc(made, 1)
                    break
                cast.then_inc(done, 1)
                eng.wait_ge(done, n + 2 * i + 1)
                ops.tensor_tensor(q, q, part[:, i, :, cols], ALU.subtract).then_inc(done, 1)

        def normalise(eng, ops, unit, norm, k):
            tt = 2 * unit.half + k
            eng.wait_ge(rstd_made[norm], unit.count(1, 1))
            eng.sem_inc(passed, 1)
            ops.tensor_scalar(xr[:, tt, :], xr[:, tt, :], mv[:, tt, 0:1], rstd[:, tt:tt + 1],
                              ALU.subtract, ALU.mult).then_inc(ln_done[norm], 1)

        def count_wins(eng, ops, unit, t):
            eng.wait_ge(compared, unit.count(2, t + 1))
            eng.wait_ge(sparse_made, unit.count(2, t))
            m01, m23, m02, m13, m03, m12 = (beats[:, k, :] for k in range(6))
            ops.tensor_tensor(wins[:, 0, :], m02, m03, ALU.add)
            ops.tensor_tensor(wins[:, 1, :], m13, m12, ALU.add)
            ops.tensor_tensor(wins[:, 2, :], m02, m12, ALU.add)
            ops.tensor_tensor(wins[:, 3, :], m03, m13, ALU.add).then_inc(wins_step, 1)
            eng.wait_ge(wins_step, unit.count(2, t + 1))
            ops.tensor_tensor(wins[:, 0, :], wins[:, 0, :], m01, ALU.add)
            ops.tensor_tensor(wins[:, 1, :], wins[:, 1, :], m01, ALU.subtract)
            ops.tensor_tensor(wins[:, 2, :], m23, wins[:, 2, :], ALU.subtract)
            ops.tensor_tensor(wins[:, 3, :], wins[:, 3, :], m23, ALU.add).then_inc(wins_made, 1)

        @block.sync
        def _(sp):
            sp.dma_start(wqkv_sb[:], wqkv).then_inc(early_in, 16)
            sp.dma_start(xT_sb, xT[0]).then_inc(xT_in, 16)
            for dst, src in ((id_f, ident), (cos_sb, cos), (sin_sb, sin)):
                sp.dma_start(dst[:], src).then_inc(early_in, 16)
            for dst, src in ((wo_sb[:], wo), (gu_in(0), wg), (gu_in(1), wu), (wd_sb[:], wd)):
                sp.dma_start(dst, src).then_inc(weights_in, 16)

            def send_q(b, half, i):
                for j in range(PARTS):
                    row = 24 * i + 8 * j
                    sp.dma_start(q_stack[b.parity][row:row + 8, 16 * half:16 * half + 16, :],
                                 part_T[:, PT_ORDER.index((i, half)), :]).then_inc(stack_in[half], 16)

            def send_k(b, half, j):
                for i in range(PARTS):
                    row = 24 * i + 8 * j
                    sp.dma_start(k_stack[b.parity][row:row + 8, 4 * half:4 * half + 4, :],
                                 part_T[32 * half:32 * half + 32, PT_ORDER.index((j, 2)), :]).then_inc(stack_in[half], 16)

            def move_x(unit, store):
                sl = slice(2 * unit.half, 2 * unit.half + 2)
                dram = (out if store else x)[unit.batch.index].rearrange("(t p) d -> p t d", p=P)[:, sl, :]
                if store:
                    sp.wait_ge(ln_done[1], unit.count(2, 2))
                    sp.dma_start(dram, xr[:, sl, :]).then_inc(out_done, 16)
                else:
                    sp.wait_ge(out_done, unit.count(16, -16))
                    sp.dma_start(xr[:, sl, :], dram).then_inc(x_in, 16)

            def move_maxima(step, b, q):
                sp.wait_ge(mb_read, mb_count(step, f"mt{q}"))
                hf, hh = q // 2, q % 2
                sp.dma_start(q_stack[b.parity][AUG:AUG + 3, 16 * hh:16 * hh + 16, HALF * hf:HALF * hf + HALF],
                             neg_T[:, q % 2, :]).then_inc(aug_in[q % 2], 16)

            for step in steps(sp):
                bA, bM, bB, bF = (step.plus(LAG[s]) for s in "AMBF")
                if bF.real:
                    move_x(Unit(bF, 1), False)
                if bB.real:
                    move_maxima(step, bB, 1)
                if bF.real:
                    move_x(Unit(bF, 0), True)
                if bA.real:
                    if bA.first < 2 and bA.r is None:
                        sp.wait_ge(stack_set[bA.first], 2)
                    sp.wait_ge(pv_done, bA.plus(-2).count(32, 32))
                    sp.wait_ge(mb_read, mb_count(step, "pT0"))
                    send_q(bA, 0, 0)
                    send_q(bA, 0, 1)
                    sp.wait_ge(mb_read, mb_count(step, "pT1"))
                    send_q(bA, 0, 2)
                    send_k(bA, 0, 0)
                if bB.real:
                    move_maxima(step, bB, 2)
                if bA.real:
                    sp.wait_ge(mb_read, mb_count(step, "pT2"))
                    send_k(bA, 0, 1)
                    send_k(bA, 0, 2)
                    for j in range(PARTS):
                        send_k(bA, 1, j)
                if bB.real:
                    move_x(Unit(bB, 0), False)
                if bA.real:
                    sp.wait_ge(mb_read, mb_count(step, "pT3"))
                    send_q(bA, 1, 0)
                    send_q(bA, 1, 1)
                    sp.wait_ge(mb_read, mb_count(step, "pT4"))
                    send_q(bA, 1, 2)
                if bA.plus(1).real:
                    sp.wait_ge(mb_filled, mb_count(step, "pT4"))
                    sp.dma_start(xT_sb, xT[bA.plus(1).index]).then_inc(xT_in, 16)
                if bB.real:
                    move_maxima(step, bB, 3)
                if bF.real:
                    move_x(Unit(bF, 1), True)
                if bM.real:
                    move_maxima(step, bM, 0)
            sp.wait_ge(out_done, 32 * B)

        @block.tensor
        def _(pe):
            pe.wait_ge(early_in, 16 * 4)

            def max_scores(b, n):
                head, qt = max_tile(n)
                if n == 0:
                    pe.wait_ge(stack_in[0], b.count(288, 288))
                if n == 32:
                    pe.wait_ge(stack_in[1], b.count(288, 288))
                pe.wait_ge(maxed, b.count(128, n - 1))
                nc.tensor.matmul(ps_m[:, n % 2, :], q_stack[b.parity][0:AUG, head, qt * P:(qt + 1) * P],
                                 k_stack[b.parity][0:AUG, head // 4, :], start=True, stop=True).then_inc(scored, 1)

            def key_scores(step, slot, i):
                b = step.plus(LAG["B"])
                g, pair, kt, hf = key_tile(slot, i)
                n = 4 * slot + i
                head = 4 * g + 2 * pair
                if slot % 8 == 0 and i == 0:
                    pe.wait_ge(aug_in[slot // 8 % 2], b.count(32, 16 * (slot // 16 + 1)))
                pe.wait_ge(exp_done, b.count(128, n - 1))
                nc.tensor.matmul(ps_s[:, n % 2, :], k_stack[b.parity][0:AUG + 3, g, kt * P:(kt + 1) * P],
                                 q_stack[b.parity][0:AUG + 3, head:head + 2, HALF * hf:HALF * hf + HALF],
                                 start=True, stop=True).then_inc(st_ready, 1)

            def values(step, quad):
                b = step.plus(LAG["B"])
                if quad == 0:
                    pe.wait_ge(v_built, b.count(1, 1))
                if quad % 4 == 0:
                    pe.wait_ge(oT_copied, b.count(8, quad // 4))
                pe.wait_ge(exp_done, b.count(128, 4 * quad + 4))
                for i in range(4):
                    g, pair, kt, hf = key_tile(quad, i)
                    mm = nc.tensor.matmul(ps_o[32 * i:32 * i + 32, :], v_aug[b.parity][:, kt, g, :],
                                          prob[:, (4 * quad + i) % 8, :], start=(kt == 0), stop=(kt == 3))
                mm.then_inc(pv_done, 1)

            def side_mb(step, name, b):
                if not (name.startswith("qkv") and b.r is None and b.first == 0):
                    pe.wait_ge(mb_read, mb_count(step, name) - 1)
                if name.startswith("ott"):
                    g = int(name[3:])
                    pe.wait_ge(oT_copied, b.count(8, g + 1))
                    for t in range(2):
                        for h in range(2):
                            mm = nc.tensor.transpose(mb[:, (2 * t + h) * P:(2 * t + h + 1) * P],
                                                     oT_sb[:, (2 * h + t) * P:(2 * h + t + 1) * P], id_f[:])
                elif name.startswith("oT"):
                    half = int(name[2:])
                    pe.wait_ge(mb_read, mb_count(step, "ott7" if half else "ott3"))
                    for kc in range(KC):
                        for t in range(2):
                            mm = nc.tensor.transpose(mb[:, (2 * kc + t) * P:(2 * kc + t + 1) * P],
                                                     o_sb[:, t, kc * P:(kc + 1) * P], id_f[:])
                elif name.startswith("xT"):
                    half = int(name[2:])
                    pe.wait_ge(ln_done[0], Unit(b, half).count(2, 2))
                    for kc in range(KC):
                        for t in range(2):
                            mm = nc.tensor.transpose(mb[:, (2 * kc + t) * P:(2 * kc + t + 1) * P],
                                                     xr[:, 2 * half + t, kc * P:(kc + 1) * P], id_f[:])
                elif name.startswith("qkv"):
                    tt = int(name[3:])
                    pe.wait_ge(xT_in, b.count(16, 16))
                    for kc in range(KC):
                        mm = nc.tensor.matmul(qkv_bank(b, tt)[:, 0:QKV], xT_sb[:, kc, tt * P:(tt + 1) * P], wqkv_sb[:, kc, :],
                                              start=(kc == 0), stop=(kc == KC - 1))
                elif name.startswith("pT"):
                    u = int(name[2:])
                    pe.wait_ge(consts_set, 2)
                    if not (b.r is None and b.first == 0) or u > 0:
                        pe.wait_ge(parts_made, b.count(1, 1))
                    if b.r is None and b.first == 0:
                        pe.wait_ge(first_q, 1 if u < 3 else 2)
                    pe.sem_inc(passed, 1)
                    for k, (i, c) in enumerate(PT_ORDER[2 * u:2 * u + 2]):
                        w = P if c < 2 else KV * HD
                        for tt in range(TT):
                            mm = nc.tensor.transpose(mb_b[0:w, k * S + tt * P:k * S + (tt + 1) * P],
                                                     part[:, i, tt, c * P:c * P + w], id_b[:])
                else:
                    q = int(name[2:])
                    pe.wait_ge(neg_made, b.count(4, q + 1))
                    pe.sem_inc(passed, 1)
                    for qt in range(2):
                        mm = nc.tensor.transpose(mb_b[0:PARTS * H // 2, qt * P:(qt + 1) * P],
                                                 neg_part[:, qt, :, :].rearrange("p a h -> p (a h)"), id_b[:])
                mm.then_inc(mb_filled, 1)

            def project(step, unit, i):
                t, kc = i // 2, i % 2
                if i == 0:
                    pe.wait_ge(weights_in, 16 * 4)
                    pe.wait_ge(ma_read, ma_free(unit, "wo"))
                    pe.wait_ge(mb_read, mb_count(step, f"oT{unit.half}"))
                mm = nc.tensor.matmul(ma[:, ma_bank(unit, "wo"), t * D:(t + 1) * D], attn_T[:, kc, t * P:(t + 1) * P],
                                      wo_sb[:, kc, :], start=(kc == 0), stop=(kc == KC - 1))
                if i == 3:
                    mm.then_inc(ma_filled, 1)

            def gate_up(step, unit, f, i):
                kc = i % 2
                if i == 0:
                    pe.wait_ge(ma_read, ma_free(unit, f"gu{f}"))
                if f == 0 and i == 0:
                    pe.wait_ge(mb_read, mb_count(step, f"xT{unit.half}"))
                    pe.wait_ge(weights_split, 2)
                w, r = wgu_sb, i // 2
                out_ = ma[:, ma_bank(unit, f"gu{f}"), r * HALF:(r + 1) * HALF]
                high, rest = feat_high[:, kc, :], feat_rest[:, kc, :]
                nc.tensor.matmul(out_, w[:, 0, r, kc, f, :], rest, start=(kc == 0), stop=False)
                nc.tensor.matmul(out_, w[:, 1, r, kc, f, :], high, start=False, stop=False)
                mm = nc.tensor.matmul(out_, w[:, 0, r, kc, f, :], high, start=False, stop=(kc == KC - 1))
                if i == 3:
                    mm.then_inc(ma_filled, 1)

            def down(unit, k):
                t, n = k // 8, k % 8
                if k == 0:
                    pe.wait_ge(ma_read, ma_free(unit, "dn"))
                if k in (0, 4):
                    pe.wait_ge(sparse_made, unit.count(2, k // 4 + 1))
                mm = nc.tensor.matmul(ma[:, ma_bank(unit, "dn"), t * D:(t + 1) * D], hid[:, n, t * P:(t + 1) * P],
                                      wd_sb[:, n, :], start=(n == 0), stop=(n == 7))
                if k == 15:
                    mm.then_inc(ma_filled, 1)

            for step in steps(pe):
                bM, bB = step.plus(LAG["M"]), step.plus(LAG["B"])
                for slot in range(SLOTS):
                    for i in range(4):
                        if bB.real:
                            key_scores(step, slot, i)
                        if slot < SLOTS - LEAD and bB.real:
                            max_scores(bB, 4 * (slot + LEAD) + i)
                        if slot >= SLOTS - LEAD and bM.real:
                            max_scores(bM, 4 * (slot + LEAD - SLOTS) + i)
                        for unit, at in units(step, slot):
                            if at == WO_AT:
                                project(step, unit, i)
                            if GU_AT <= at < GU_AT + 8:
                                gate_up(step, unit, at - GU_AT, i)
                            if DN_AT <= at < DN_END and (i < 3 or at == DN_END - 1):
                                down(unit, 3 * (at - DN_AT) + i)
                        for at, name, stage in MB_USES:
                            b = step.plus(LAG[stage])
                            if at == (slot, i) and b.real:
                                side_mb(step, name, b)
                    if bB.real and slot >= 1:
                        values(step, slot - 1)
                if bB.real:
                    values(step, SLOTS - 1)

        @block.scalar
        def _(act):
            act.wait_ge(early_in, 16 * 4)

            def exps(step, slot, i):
                b = step.plus(LAG["B"])
                n = 4 * slot + i
                if i == 0:
                    act.wait_ge(pv_done, b.count(32, slot - 1))
                if n == 0 and b.r is None and b.first == 0:
                    act.wait_ge(weights_split, 2)
                act.wait_ge(st_ready, b.count(128, n + 1))
                nc.scalar.activation(prob[:, n % 8, :], ps_s[:, n % 2, :], ACT.Exp, scale=SCALE).then_inc(exp_done, 1)

            def output_copy(b, g, last_use):
                act.wait_ge(pv_done, b.count(32, 4 * g + 4))
                if last_use is not None:
                    act.wait_ge(mb_filled, last_use)
                nc.scalar.copy(oT_sb[:], ps_o[:]).then_inc(oT_copied, 1)

            def side(step, slot, i):
                for at, name, stage in MB_USES:
                    b = step.plus(LAG[stage])
                    if at != (slot, i) or not b.real or name.startswith("ott"):
                        continue
                    act.wait_ge(mb_filled, mb_count(step, name))
                    if name.startswith("qkv"):
                        tt = int(name[3:])
                        if tt == 0:
                            act.wait_ge(parts_made, b.count(1, 0))
                            act.wait_ge(stack_in[0], b.count(288, 0))
                            act.wait_ge(stack_in[1], b.count(288, 0))
                            act.wait_ge(v_built, b.count(1, 0))
                        nc.scalar.copy(v_raw[:, tt, :], qkv_bank(b, tt)[:, QK:QKV])
                        nc.scalar.copy(qk_of(b)[:, tt, :], qkv_bank(b, tt)[:, 0:QK]).then_inc(mb_read, 1)
                    elif name.startswith("pT"):
                        u = int(name[2:])
                        chunks = PT_ORDER[2 * u:2 * u + 2]
                        if len({c < 2 for _, c in chunks}) == 1:
                            w = P if chunks[0][1] < 2 else KV * HD
                            cp = nc.scalar.copy(part_T[0:w, 2 * u:2 * u + len(chunks), :],
                                                mb_b[0:w, 0:len(chunks) * S].rearrange("p (k t) -> p k t", t=S))
                            cp.then_inc(mb_read, 1)
                        else:
                            nc.scalar.copy(part_T[0:P, 2 * u, :], mb_b[0:P, 0:S])
                            nc.scalar.copy(part_T[0:KV * HD, 2 * u + 1, :], mb_b[0:KV * HD, S:2 * S]).then_inc(mb_read, 1)
                    elif name.startswith("mt"):
                        q = int(name[2:])
                        act.wait_ge(aug_in[q % 2], b.count(32, 16 * (q // 2)))
                        n = PARTS * H // 2
                        nc.scalar.copy(neg_T[:, q % 2, :], mb_b[0:n, 0:HALF]).then_inc(mb_read, 1)
                    else:
                        unit = Unit(b, int(name[2:]))
                        if name.startswith("xT"):
                            act.wait_ge(ma_filled, ma_free(unit, "gu0"))
                            nc.scalar.copy(feat_high[:].rearrange("p k t -> p (k t)"), mb[:, :]).then_inc(high_made, 1)
                        else:
                            act.wait_ge(ma_read, unit.count(10, -1))
                            nc.scalar.copy(attn_T[:].rearrange("p k t -> p (k t)"), mb[:, :]).then_inc(mb_read, 1)

            for step in steps(act):
                bB, bF = step.plus(LAG["B"]), step.plus(LAG["F"])
                for slot in range(SLOTS):
                    if slot == 1 and bF.real:
                        output_copy(bF, 7, mb_count(step.plus(-1), "ott6"))
                    if slot % 4 == 1 and slot >= 5 and bB.real:
                        g = slot // 4 - 1
                        prev = f"ott{g - 1}" if g else "ott7"
                        output_copy(bB, g, mb_count(step, prev) if g or bF.real else None)
                    for i in range(4):
                        if bB.real:
                            exps(step, slot, i)
                        for unit, at in units(step, slot):
                            if i == 0 and GU_AT < at <= GU_AT + 8:
                                f = at - GU_AT - 1
                                act.wait_ge(ma_filled, ma_count(unit, f"gu{f}"))
                                nc.scalar.activation(gate[:, f % 2, :], ma[:, ma_bank(unit, f"gu{f}"), 0:HALF], ACT.Tanh,
                                                     scale=0.5).then_inc(tanh_done, 1)
                            if i == 3 and at in MAG_AT:
                                t = MAG_AT.index(at)
                                act.wait_ge(ma_read, ma_count(unit, f"gu{4 * t + 3}"))
                                act.wait_ge(compared, unit.count(2, t))
                                nc.scalar.activation(mag[:], hid[:, 4 * t:4 * t + 4, :], ACT.Abs).then_inc(mag_made, 1)
                        side(step, slot, i)
                    if step.r is None and step.first == -1 and slot == 16:
                        nc.scalar.mul(q_stack[1][:].bitcast(F32).rearrange("p h t -> p (h t)"),
                                      id_f[:, 0:1].broadcast_to([P, H * S // 2]), 0.0).then_inc(stack_set[1], 1)

        @block.vector
        def _(dve):
            for n in range(2):
                nc.vector.memset(k_stack[n][:].bitcast(F32), 0.0).then_inc(zeroed, 1)
            for n in range(2):
                dve.wait_ge(zeroed, n + 1)
                nc.vector.memset(k_stack[n][AUG:AUG + 3, :, :], 1.0).then_inc(stack_set[n], 1)
            dve.wait_ge(early_in, 16 * 4)
            nc.vector.tensor_copy(id_b[:], id_f[:]).then_inc(consts_set, 1)

            def row_maximum(b, n):
                head, qt = max_tile(n)
                q = n // 32
                if n % 32 == 0:
                    dve.wait_ge(neg_made, b.count(4, q - 1))
                dve.wait_ge(scored, b.count(128, n + 1))
                nc.vector.tensor_reduce(row_max[:, q % 2, qt % 2, head % 16:head % 16 + 1], ps_m[:, n % 2, :],
                                        AX.X, ALU.max).then_inc(maxed, 1)

            def normalise_group(step, b, name):
                g = int(name[3:])
                dve.wait_ge(mb_filled, mb_count(step, name))
                t = mb[:, :].rearrange("p (t i c) -> p t i c", t=2, i=8)
                nc.vector.reciprocal(recip[:], t[:, :, :, HD]).then_inc(recip_made, 1)
                dve.wait_ge(recip_made, b.count(8, g + 1))
                o = o_sb[:, :, 64 * (g % 4):64 * (g % 4) + 64].rearrange("p t (i d) -> p t i d", i=8)
                nc.vector.tensor_tensor(o, t[:, :, :, 0:HD], recip[:].unsqueeze(3).broadcast_to([P, 2, 8, HD]),
                                        ALU.mult).then_inc(mb_read, 1)

            def residual(unit, norm, name):
                dve.wait_ge(ma_filled, ma_count(unit, name))
                sl = xr[:, 2 * unit.half:2 * unit.half + 2, :]
                nc.vector.tensor_tensor(sl, ma[:, ma_bank(unit, name), :].rearrange("p (k d) -> p k d", k=2), sl,
                                        ALU.add).then_inc(ma_read, 1)

            def statistics(unit, norm, name, k):
                tt = 2 * unit.half + k
                dve.wait_ge(ma_read, ma_count(unit, name))
                nc.vector.bn_stats(stats[:, tt, :], xr[:, tt, :]).then_inc(summed[norm], 1)
                dve.wait_ge(summed[norm], unit.count(2, k + 1))
                dve.sem_inc(passed, 1)
                nc.vector.bn_aggr(mv[:, tt, :], stats[:, tt, :]).then_inc(stat_made[norm], 1)

            def swiglu(unit, f):
                dve.wait_ge(tanh_done, unit.count(8, f + 1))
                g, bank = gate[:, f % 2, :], ma_bank(unit, f"gu{f}")
                nc.vector.scalar_tensor_tensor(out=g, in0=g, scalar=1.0, in1=ma[:, bank, 0:HALF],
                                               op0=ALU.add, op1=ALU.mult).then_inc(gate_made, 1)
                dve.wait_ge(gate_made, unit.count(8, f + 1))
                nc.vector.scalar_tensor_tensor(out=hid[:, f, :], in0=g, scalar=0.5, in1=ma[:, bank, HALF:2 * HALF],
                                               op0=ALU.mult, op1=ALU.mult).then_inc(ma_read, 1)

            def compare(unit, t, piece):
                if piece == 0:
                    dve.wait_ge(mag_made, unit.count(2, t + 1))
                    dve.wait_ge(wins_made, unit.count(2, t))
                    nc.vector.tensor_tensor(beats[:, 0:2, :], mag[:, 0:4:2, :], mag[:, 1:4:2, :], ALU.is_ge)
                elif piece == 1:
                    nc.vector.tensor_tensor(beats[:, 2:4, :], mag[:, 0:2, :], mag[:, 2:4, :], ALU.is_ge)
                else:
                    nc.vector.tensor_tensor(beats[:, 4, :], mag[:, 0, :], mag[:, 3, :], ALU.is_ge)
                    nc.vector.tensor_tensor(beats[:, 5, :], mag[:, 1, :], mag[:, 2, :], ALU.is_ge).then_inc(compared, 1)

            def sparsify(unit, t, j):
                if j == 0:
                    dve.wait_ge(wins_made, unit.count(2, t + 1))
                op, bound = ((ALU.is_ge, 2.0), (ALU.is_ge, 1.0), (ALU.is_ge, 0.0), (ALU.is_le, 1.0))[j]
                h = hid[:, 4 * t + j, :]
                last = nc.vector.scalar_tensor_tensor(out=h, in0=wins[:, j, :], scalar=bound, in1=h,
                                                      op0=op, op1=ALU.mult)
                if j == 3:
                    last.then_inc(sparse_made, 1)

            for step in steps(dve):
                bM, bB, bF = (step.plus(LAG[s]) for s in "MBF")
                if step.r is None and step.first == -1:
                    dve.wait_ge(mb_read, mb_count(step, "qkv3"))
                    for half in range(2):
                        rotate(dve, nc.vector, qk_of(step.plus(1)), half, first_q_step, 7 * half)
                        split(dve, nc.vector, qk_of(step.plus(1)), slice(P * half, P * half + P), first_q_step, 7 * half + 3, first_q)
                for slot in range(SLOTS):
                    for i in range(4):
                        if slot < SLOTS - LEAD and bB.real:
                            row_maximum(bB, 4 * (slot + LEAD) + i)
                        if slot >= SLOTS - LEAD and bM.real:
                            row_maximum(bM, 4 * (slot + LEAD - SLOTS) + i)
                        for at, name, stage in MB_USES:
                            b = step.plus(LAG[stage])
                            if at == (slot, i) and b.real and name.startswith("ott"):
                                if name == "ott0" and bF.real:
                                    dve.wait_ge(mb_filled, mb_count(step, "oT1"))
                                if name == "ott4":
                                    dve.wait_ge(mb_filled, mb_count(step, "oT0"))
                                normalise_group(step, b, name)
                        for unit, at in units(step, slot):
                            if i == 1 and at == REST_AT:
                                dve.wait_ge(high_made, unit.count(1, 1))
                                nc.vector.tensor_tensor(feat_rest[:].rearrange("p k t -> p (k t)"), mb[:, :],
                                                        feat_high[:].rearrange("p k t -> p (k t)").bitcast(F32), ALU.subtract).then_inc(mb_read, 1)
                            if i == 1 and at == NORM_AT:
                                dve.wait_ge(x_in, unit.count(16, 16))
                                residual(unit, 0, "wo")
                            if i >= 2 and at == NORM_AT:
                                statistics(unit, 0, "wo", i - 2)
                            if i in (1, 2) and at == NORM_AT + 1:
                                normalise(dve, nc.vector, unit, 0, i - 1)
                            if i == 1 and GU_AT < at <= GU_AT + 8:
                                swiglu(unit, at - GU_AT - 1)
                            for t in range(2):
                                if (at, i) in COMPARE_AT[t]:
                                    compare(unit, t, COMPARE_AT[t].index((at, i)))
                                if (at, i) == COMPARE_AT[t][-1] and unit.alone:
                                    count_wins(dve, nc.vector, unit, t)
                                    for j in range(4):
                                        sparsify(unit, t, j)
                                if (at, i) in SPARSE_AT[t] and not unit.alone:
                                    sparsify(unit, t, SPARSE_AT[t].index((at, i)))
                            if i == 1 and at == DN_END:
                                residual(unit, 1, "dn")
                            if i >= 2 and at == DN_END:
                                statistics(unit, 1, "dn", i - 2)
                            if i in (1, 2) and at == DN_END + 1 and unit.alone:
                                normalise(dve, nc.vector, unit, 1, i - 1)

        @block.gpsimd
        def _(pool):
            for n in range(2):
                nc.gpsimd.memset(v_aug[n][:], 0.0).then_inc(v_zeroed, 1)
            nc.gpsimd.memset(half_neg[:], -0.5)
            nc.gpsimd.memset(q_stack[0][:].bitcast(F32), 0.0).then_inc(stack_set[0], 1)
            pool.wait_ge(v_zeroed, 2)
            nc.gpsimd.memset(v_aug[0][:, :, :, HD:HD + 1], 1.0)
            nc.gpsimd.memset(v_aug[1][:, :, :, HD:HD + 1], 1.0).then_inc(consts_set, 1)
            pool.wait_ge(early_in, 16 * 4)

            def build_v(step, b):
                pool.wait_ge(mb_read, mb_count(step, "qkv3"))
                pool.wait_ge(pv_done, b.plus(-2).count(32, 32))
                pool.sem_inc(passed, 1)
                nc.gpsimd.tensor_copy(v_aug[b.parity][:, :, :, 0:HD],
                                      v_raw[:].rearrange("p t (k d) -> p t k d", d=HD)).then_inc(v_built, 1)

            def split_negated(b, q, last_transposed):
                m = row_max[:, q % 2]
                if last_transposed is not None:
                    pool.wait_ge(mb_filled, last_transposed)
                pool.wait_ge(maxed, b.count(128, 32 * (q + 1)))
                pool.sem_inc(passed, 1)
                k = 4 * q
                nc.gpsimd.tensor_scalar(neg_part[:, :, 0, :], m, -1.0, None, ALU.mult).then_inc(neg_step, 1)
                pool.wait_ge(neg_step, b.count(16, k + 1))
                nc.gpsimd.tensor_tensor(max_rest[:], m, neg_part[:, :, 0, :], ALU.add).then_inc(neg_step, 1)
                pool.wait_ge(neg_step, b.count(16, k + 2))
                pool.sem_inc(passed, 1)
                nc.gpsimd.tensor_scalar(neg_part[:, :, 1, :], max_rest[:], -1.0, None, ALU.mult).then_inc(neg_step, 1)
                pool.wait_ge(neg_step, b.count(16, k + 3))
                nc.gpsimd.tensor_tensor(max_rest[:], max_rest[:], neg_part[:, :, 1, :], ALU.add).then_inc(neg_step, 1)
                pool.wait_ge(neg_step, b.count(16, k + 4))
                pool.sem_inc(passed, 1)
                nc.gpsimd.tensor_scalar(neg_part[:, :, 2, :], max_rest[:], -1.0, None, ALU.mult).then_inc(neg_made, 1)

            def inverse_std(unit, norm):
                pool.wait_ge(stat_made[norm], unit.count(2, 2))
                pool.sem_inc(passed, 1)
                sl = slice(2 * unit.half, 2 * unit.half + 2)
                nc.gpsimd.tensor_scalar(var_eps[:, sl], mv[:, sl, 1], EPS, None, ALU.add).then_inc(var_made[norm], 1)
                pool.wait_ge(var_made[norm], unit.count(1, 1))
                nc.gpsimd.tensor_tensor(rstd[:, sl], var_eps[:, sl], half_neg[:], ALU.pow).then_inc(rstd_made[norm], 1)

            for step in steps(pool):
                bA, bM, bB = (step.plus(LAG[s]) for s in "AMB")
                for slot in range(SLOTS):
                    if slot == 4 and bB.real:
                        split_negated(bB, 1, mb_count(step.plus(-1), "mt0"))
                    if slot in (12, 20) and bB.real:
                        split_negated(bB, slot // 8 + 1, mb_count(step, f"mt{slot // 8}"))
                    if slot == 28 and bM.real:
                        split_negated(bM, 0, mb_count(step, "mt3") if bB.real else None)
                    for unit, at in units(step, slot):
                        if at == NORM_AT:
                            inverse_std(unit, 0)
                        if at in WINS_AT and not unit.alone:
                            count_wins(pool, nc.gpsimd, unit, WINS_AT.index(at))
                        if at == DN_END:
                            inverse_std(unit, 1)
                            if not unit.alone:
                                for k in range(2):
                                    normalise(pool, nc.gpsimd, unit, 1, k)
                    if bA.real and slot == 3:
                        pool.wait_ge(mb_read, mb_count(step, "qkv3"))
                    if bA.real and bA.r is None and bA.first == 0:
                        if slot == 3:
                            rotate(pool, nc.gpsimd, qk_of(bA), 2, first_k_step, 0)
                            rotate(pool, nc.gpsimd, qk_of(bA), 3, first_k_step, 3)
                            split(pool, nc.gpsimd, qk_of(bA), slice(2 * P, QK), first_k_step, 6, parts_made)
                            build_v(step, bA)
                            pool.wait_ge(weights_in, 16 * 4)
                            for r in range(2):
                                nc.gpsimd.tensor_copy(wgu_sb[:, 0, r], gu_in(r)).then_inc(weights_high, 1)
                            for r in range(2):
                                pool.wait_ge(weights_high, r + 1)
                                nc.gpsimd.tensor_tensor(wgu_sb[:, 1, r], gu_in(r), wgu_sb[:, 0, r].bitcast(F32),
                                                        ALU.subtract).then_inc(weights_split, 1)
                    elif bA.real:
                        n = bA.plus(-1).count(16, 0)
                        if 3 <= slot < 3 + len(ROPE_CHUNKS):
                            rotate(pool, nc.gpsimd, qk_of(bA), slot - 3, rot_step, n + 3 * (slot - 3))
                        if slot == 7:
                            pool.wait_ge(mb_filled, mb_count(step.plus(-1), "pT4"))
                            split(pool, nc.gpsimd, qk_of(bA), slice(0, QK), rot_step, n + 12, parts_made)
                            build_v(step, bA)


def kernel(L0_attn_x, L0_attn_Wq, L0_attn_Wk, L0_attn_Wv, L0_attn_Wo, L0_ffn_w_gate, L0_ffn_w_up, L0_ffn_w_down):
    import concourse.bacc as _bacc
    from concourse.bass_utils import run_bass_kernel_spmd as _run

    x = np.asarray(L0_attn_x)
    wq = np.asarray(L0_attn_Wq).reshape(2, H // 2, HD, D).transpose(0, 2, 1, 3).reshape(H * HD, D)
    wk = np.asarray(L0_attn_Wk).reshape(2, KV // 2, HD, D).transpose(0, 2, 1, 3).reshape(KV * HD, D)
    wqkv = np.concatenate([wq, wk, np.asarray(L0_attn_Wv)], axis=0)

    def chunks(w):
        return w.reshape(KC, P, -1).transpose(1, 0, 2)

    def hidden_tiles(w):
        return w.reshape(KC, P, 2, P, 4).transpose(1, 0, 2, 4, 3).reshape(P, KC, 8, P)

    inv = (1.0 / np.float32(10000.0) ** (np.arange(0, HD, 2, dtype=np.float32) / HD)).astype(np.float32)
    ang = np.arange(S, dtype=np.float32)[:, None] * inv[None, :]
    cos = np.concatenate([np.cos(ang), np.cos(ang)], axis=1).reshape(TT, P, HD).transpose(1, 0, 2)
    sin = np.concatenate([-np.sin(ang), np.sin(ang)], axis=1).reshape(TT, P, HD).transpose(1, 0, 2)
    data = {
        "x": x,
        "xT": x.reshape(B, S, KC, P).transpose(0, 3, 2, 1),
        "wqkv": chunks(wqkv.T),
        "wo": chunks(np.asarray(L0_attn_Wo).T.reshape(4, 4, 2, HD, D).transpose(0, 2, 1, 3, 4).reshape(D, D)),
        "wg": hidden_tiles(np.asarray(L0_ffn_w_gate)),
        "wu": hidden_tiles(np.asarray(L0_ffn_w_up)),
        "wd": np.asarray(L0_ffn_w_down).reshape(2, P, 4, D).transpose(1, 0, 2, 3).reshape(P, 8, D),
        "ident": np.eye(P, dtype=np.float32),
        "cos": cos, "sin": sin,
    }
    nc = _bacc.Bacc("TRN2", target_bir_lowering=False, num_devices=1)
    arrays, args = {}, []
    for name, a in data.items():
        a = np.ascontiguousarray(a)
        arrays[f"in_{name}"] = a
        args.append(nc.dram_tensor(f"in_{name}", a.shape, mybir.dt.from_np(a.dtype), kind="ExternalInput").ap())
    args.append(nc.dram_tensor("out_0", (B, S, D), F32, kind="ExternalOutput").ap())
    layer_kernel(nc, *args)
    return _run(nc, [arrays], core_ids=[0]).results[0]["out_0"]
```
